# Optimizing a Trainium2 kernel written in Bass

```python
import numpy as np
import jax
import jax.numpy as jnp

def _softmax(x, axis=-1):
    return jax.nn.softmax(x, axis=axis)

def _gelu(x):
    return jax.nn.gelu(x, approximate=True)

def _silu(x):
    return jax.nn.silu(x)

def _sigmoid(x):
    return jax.nn.sigmoid(x)

def _layernorm(x, axis=-1, eps=1e-05):
    m = jnp.mean(x, axis=axis, keepdims=True)
    v = jnp.var(x, axis=axis, keepdims=True)
    return (x - m) / jnp.sqrt(v + eps)

def _scatter_add(tgt, idx, src, axis=0):
    return tgt.at[idx].add(src)

def _segment_sum(src, seg, n):
    return jax.ops.segment_sum(src, seg, n)
kernel_name = 'mk_adj_resnorm_d1_adj_r2_fb7ef5'

def setup_inputs(seed: int=0):
    np.random.seed(seed)
    _w = jnp.asarray

    def _rec_inputs():
        import jax
        import jax.numpy as jnp
        _gk = jax.random.key(seed)
        x = -0.0001538 + 1 * jax.random.normal(jax.random.fold_in(_gk, 1), (128, 128, 384), jnp.float32)
        _a = jax.random.bernoulli(jax.random.fold_in(_gk, 2), 0.0625, (128, 128, 128))
        _af = _a.astype(jnp.float32)
        adj = _af
        return (x, adj)
    x, adj = _rec_inputs()

    def _L0_gnn_setup():
        import jax, jax.numpy as jnp
        import numpy as np
        LN_EPS = 1e-12

        def _digcn_forward(hidden_state, adjacency_matrix, Wl, bl, Ws, bs, Wr, br, ln_w, ln_b):
            B, S, D = hidden_state.shape
            temper = jnp.asarray(D, jnp.float32) ** 0.5
            i = jnp.arange(S)
            upper = (i[None, :] > i[:, None]).astype(hidden_state.dtype)
            lower = (i[None, :] < i[:, None]).astype(hidden_state.dtype)

            def layer(h, params):
                wl, b_l, ws, b_s, wr, b_r, g, beta = params
                u = jnp.einsum('bid,bjd->bij', h, h) / temper
                a = jax.nn.softmax(u, axis=-1)
                delta = a * adjacency_matrix
                attn = delta / (jnp.sum(delta, axis=-1, keepdims=True) + 1e-10)
                hl = h @ wl.T + b_l
                hs = h @ ws.T + b_s
                hr = h @ wr.T + b_r
                diag_a = jnp.diagonal(attn, axis1=1, axis2=2)
                ctx = jnp.einsum('bij,bjd->bid', attn * upper, hl) + diag_a[..., None] * hs + jnp.einsum('bij,bjd->bid', attn * lower, hr)
                mean = ctx.mean(-1, keepdims=True)
                var = ctx.var(-1, keepdims=True)
                o = (ctx - mean) / jnp.sqrt(var + LN_EPS) * g + beta
                return (jax.nn.relu(o), None)
            out, _ = jax.lax.scan(layer, hidden_state, (Wl, bl, Ws, bs, Wr, br, ln_w, ln_b))
            return out
        key = jax.random.key(seed)
        ks = jax.random.split(key, 6)
        B, S, D, L = (8, 512, 384, 2)
        scale = (1.0 / D) ** 0.5
        hidden_state = jax.random.normal(ks[0], (B, S, D), jnp.float32)
        adjacency_matrix = (jax.random.uniform(ks[1], (B, S, S)) < 0.05).astype(jnp.float32)
        Wl = jax.random.normal(ks[2], (L, D, D), jnp.float32) * scale
        Ws = jax.random.normal(ks[3], (L, D, D), jnp.float32) * scale
        Wr = jax.random.normal(ks[4], (L, D, D), jnp.float32) * scale
        bl = jnp.zeros((L, D), jnp.float32)
        bs = jnp.zeros((L, D), jnp.float32)
        br = jnp.zeros((L, D), jnp.float32)
        ln_w = jnp.ones((L, D), jnp.float32)
        ln_b = jnp.zeros((L, D), jnp.float32)
        return dict(hidden_state=hidden_state, adjacency_matrix=adjacency_matrix, Wl=Wl, bl=bl, Ws=Ws, bs=bs, Wr=Wr, br=br, ln_w=ln_w, ln_b=ln_b)
    _L0_gnn_all = _L0_gnn_setup()
    _L0_gnn_in = {k: v for k, v in _L0_gnn_all.items() if k in ('Wl', 'bl', 'Ws', 'bs', 'Wr', 'br', 'ln_w', 'ln_b')}
    del _L0_gnn_all
    return {'x': x, 'adj': adj, 'L0_gnn_Wl': _L0_gnn_in['Wl'], 'L0_gnn_bl': _L0_gnn_in['bl'], 'L0_gnn_Ws': _L0_gnn_in['Ws'], 'L0_gnn_bs': _L0_gnn_in['bs'], 'L0_gnn_Wr': _L0_gnn_in['Wr'], 'L0_gnn_br': _L0_gnn_in['br'], 'L0_gnn_ln_w': _L0_gnn_in['ln_w'], 'L0_gnn_ln_b': _L0_gnn_in['ln_b']}

def reference(x, adj, L0_gnn_Wl, L0_gnn_bl, L0_gnn_Ws, L0_gnn_bs, L0_gnn_Wr, L0_gnn_br, L0_gnn_ln_w, L0_gnn_ln_b):
    import jax
    import jax.numpy as jnp

    def _L0_gnn_ref(hidden_state, adjacency_matrix, Wl, bl, Ws, bs, Wr, br, ln_w, ln_b):
        import jax, jax.numpy as jnp
        import numpy as np
        LN_EPS = 1e-12

        def _digcn_forward(hidden_state, adjacency_matrix, Wl, bl, Ws, bs, Wr, br, ln_w, ln_b):
            B, S, D = hidden_state.shape
            temper = jnp.asarray(D, jnp.float32) ** 0.5
            i = jnp.arange(S)
            upper = (i[None, :] > i[:, None]).astype(hidden_state.dtype)
            lower = (i[None, :] < i[:, None]).astype(hidden_state.dtype)

            def layer(h, params):
                wl, b_l, ws, b_s, wr, b_r, g, beta = params
                u = jnp.einsum('bid,bjd->bij', h, h) / temper
                a = jax.nn.softmax(u, axis=-1)
                delta = a * adjacency_matrix
                attn = delta / (jnp.sum(delta, axis=-1, keepdims=True) + 1e-10)
                hl = h @ wl.T + b_l
                hs = h @ ws.T + b_s
                hr = h @ wr.T + b_r
                diag_a = jnp.diagonal(attn, axis1=1, axis2=2)
                ctx = jnp.einsum('bij,bjd->bid', attn * upper, hl) + diag_a[..., None] * hs + jnp.einsum('bij,bjd->bid', attn * lower, hr)
                mean = ctx.mean(-1, keepdims=True)
                var = ctx.var(-1, keepdims=True)
                o = (ctx - mean) / jnp.sqrt(var + LN_EPS) * g + beta
                return (jax.nn.relu(o), None)
            out, _ = jax.lax.scan(layer, hidden_state, (Wl, bl, Ws, bs, Wr, br, ln_w, ln_b))
            return out
        return _digcn_forward(hidden_state, adjacency_matrix, Wl, bl, Ws, bs, Wr, br, ln_w, ln_b)
    x = _layernorm(x + _L0_gnn_ref(x, adj, L0_gnn_Wl, L0_gnn_bl, L0_gnn_Ws, L0_gnn_bs, L0_gnn_Wr, L0_gnn_br, L0_gnn_ln_w, L0_gnn_ln_b), axis=-1)
    return x

_drawn_inputs = setup_inputs


def setup_inputs(seed=0):
    import zlib

    import numpy as np

    out = dict(_drawn_inputs(seed))
    spreads = {'L0_gnn_bl': (0.0, 0.1),
     'L0_gnn_bs': (0.0, 0.301),
     'L0_gnn_br': (0.0, 0.1),
     'L0_gnn_ln_w': (1.0, 0.2),
     'L0_gnn_ln_b': (0.0, 0.1)}
    factors = {}
    for name, (base, spread) in spreads.items():
        noise = np.random.default_rng([zlib.crc32(name.encode()), seed]).standard_normal(out[name].shape)
        drawn = base * np.exp(spread * noise) if base else spread * noise
        out[name] = jnp.asarray(drawn.astype(out[name].dtype))
    for name, factor in factors.items():
        out[name] = (out[name] * factor).astype(out[name].dtype)
    return out
```

```python
from contextlib import ExitStack

import concourse.bass as bass
from concourse import mybir

F32 = mybir.dt.float32
F32R = mybir.dt.float32r
ALU = mybir.AluOpType
ACT = mybir.ActivationFunctionType
AX = mybir.AxisListType

P = 128
UP, LOW, SELF = range(3)
HI, LO = range(2)
TERMS = [(HI, HI), (LO, HI), (HI, LO)]
ROWMAX, NEGMAX, EXPSUM, ADJSUM, DENOM, DENOM2, DIAG, MEAN, VAR, VEPS, RSTD, NBIAS, COLS = range(13)

ATTN_EPS = 1e-10
GNN_EPS = 1e-12
OUT_EPS = 1e-5


def graph_block(nc: bass.Bass, xT: bass.AP, x: bass.AP, adj: bass.AP, WT: bass.AP, bias: bass.AP,
                gain_cols: bass.AP, shift_cols: bass.AP, gain_row: bass.AP, shift_row: bass.AP, out: bass.AP):
    G, N, D = x.shape
    C = D // P
    assert N == P and D == C * P and G % 2 == 0 and G >= 12
    SCALE = float(D) ** -0.5
    FIRST, LAST = 4, G - 4
    END = G + 4

    with ExitStack() as ctx:
        def sb(name, shape, dtype=F32):
            return ctx.enter_context(nc.sbuf_tensor(name, shape, dtype))

        def bank(name, shape):
            return ctx.enter_context(nc.psum_tensor(name, shape, F32))

        def sem(name):
            return ctx.enter_context(nc.semaphore(name))

        w_raw = sb("w_raw", [P, 2, 3, C, D])
        w = sb("w", [P, 2, 3, 2, C, D], F32R)
        bias_all = sb("bias_all", [P, 2, 3, D])
        gain1 = sb("gain1", [P, C])
        shift1 = sb("shift1", [P, C])
        gain2 = sb("gain2", [P, D])
        shift2 = sb("shift2", [P, D])
        ident = sb("ident", [P, P])
        sides = sb("sides", [P, 2, P])
        neg_half = sb("neg_half", [P, 1])
        xt_raw = sb("xt_raw", [P, 2, C, N])
        xn = sb("xn", [P, 2, D])
        adj_tile = [sb("adj_layer1", [P, 2, N]), sb("adj_layer2", [P, 2, N])]
        hT = [sb("hT_layer1", [P, 2, 2, C, N], F32R), sb("hT_layer2", [P, 2, 2, C, N], F32R)]
        relu_T = sb("relu_T", [P, C, N])
        E = [sb(f"exps{k}", [P, N]) for k in (1, 2)]
        A = [sb(f"attn{k}", [P, N]) for k in (1, 2)]
        diag_scratch = [sb(f"diag_scratch{k}", [P, N]) for k in (1, 2)]
        AT = [sb(f"attnT{k}", [P, 2, N]) for k in (1, 2)]
        AT_split = [sb(f"attnT_split{k}", [P, 2, 2, N], F32R) for k in (1, 2)]
        proj = [sb(f"proj{k}", [P, 3, D]) for k in (1, 2)]
        proj_split = [sb(f"proj_split{k}", [P, 2, 2, D], F32R) for k in (1, 2)]
        gathered = [sb(f"gathered{k}", [P, D]) for k in (1, 2)]
        normed = [sb(f"normed{k}", [P, D]) for k in (1, 2)]
        stats6 = [sb(f"stats6_{k}", [P, 6]) for k in (1, 2)]
        rows = [sb(f"rows{k}", [P, 2, COLS]) for k in (1, 2)]
        scaled = sb("scaled", [P, D])
        shifted = sb("shifted", [P, D])
        y = sb("y", [P, D])
        y_stats6 = sb("y_stats6", [P, 6])
        y_rows = sb("y_rows", [P, 2, COLS])
        o = sb("o", [P, 2, D])

        p_proj = bank("p_proj", [P, 3, 512])
        p_gather = [bank("p_gather1", [P, 512]), bank("p_gather2", [P, 512])]
        p_score = [bank("p_score1", [P, 512])[:, 0:N], bank("p_score2", [P, 512])[:, 0:N]]
        p_attnT = bank("p_attnT", [P, 512])[:, 0:N]

        s_w = [sem("s_w1"), sem("s_w2")]
        s_const = sem("s_const")
        s_xt = [sem("s_xt_even"), sem("s_xt_odd")]
        s_xn = [sem("s_xn_even"), sem("s_xn_odd")]
        s_adj = [[sem("s_adj1_even"), sem("s_adj1_odd")], [sem("s_adj2_even"), sem("s_adj2_odd")]]
        s_out = [sem("s_out_even"), sem("s_out_odd")]
        s_setup = sem("s_setup")
        s_w_hi = [sem("s_w_hi1"), sem("s_w_hi2")]
        s_w_lo = [sem("s_w_lo1"), sem("s_w_lo2")]

        def per_layer(name):
            return [sem(f"{name}1"), sem(f"{name}2")]

        s_hi = per_layer("s_hi")
        s_lo = per_layer("s_lo")
        s_score = per_layer("s_score")
        s_rowmax = per_layer("s_rowmax")
        s_negmax = per_layer("s_negmax")
        s_exp = per_layer("s_exp")
        s_attn = per_layer("s_attn")
        s_diag = per_layer("s_diag")
        s_denom = per_layer("s_denom")
        s_denom2 = per_layer("s_denom2")
        s_attnT = per_layer("s_attnT")
        s_side = per_layer("s_side")
        s_side_hi = per_layer("s_side_hi")
        s_side_lo = per_layer("s_side_lo")
        s_proj = per_layer("s_proj")
        s_self = per_layer("s_self")
        s_biased = per_layer("s_biased")
        s_self_biased = per_layer("s_self_biased")
        s_proj_hi = per_layer("s_proj_hi")
        s_proj_lo = per_layer("s_proj_lo")
        s_gather = per_layer("s_gather")
        s_whole = per_layer("s_whole")
        s_stats = per_layer("s_stats")
        s_moments = per_layer("s_moments")
        s_veps = per_layer("s_veps")
        s_rstd = per_layer("s_rstd")
        s_nbias = per_layer("s_nbias")
        s_normed = per_layer("s_normed")
        s_normedT = sem("s_normedT")
        s_relu = sem("s_relu")
        s_scaled = sem("s_scaled")
        s_shifted = sem("s_shifted")
        s_y = sem("s_y")
        s_y_stats = sem("s_y_stats")
        s_y_moments = sem("s_y_moments")
        s_y_veps = sem("s_y_veps")
        s_y_rstd = sem("s_y_rstd")
        s_y_nbias = sem("s_y_nbias")
        s_o = sem("s_o")

        def live(i, b):
            return not isinstance(i, int) or 0 <= b < G

        def done(eng, s, b):
            if not isinstance(b, int) or b >= 0:
                eng.wait_ge(s, b + 1)

        def moved(eng, pair, b, slot):
            if not isinstance(b, int) or b >= 0:
                eng.wait_ge(pair[slot], (b - slot) * 8 + 16)

        def own_wait(eng):
            eng.wait_ge(s_setup, 5)

        def run(eng, iteration):
            for i in range(FIRST):
                iteration(i, i % 2)
            with eng.Fori(FIRST, LAST, 2) as i:
                iteration(i, 0)
                iteration(i + 1, 1)
            for i in range(LAST, END):
                iteration(i, i % 2)

        def col(tile, slot, k):
            return tile[:, slot, k:k + 1]

        block = ctx.enter_context(nc.Block())

        @block.sync
        def _(sp):
            for b in (0, 1, 2):
                if b == 2:
                    done(sp, s_lo[0], 0)
                sp.dma_start(xt_raw[:, b % 2], xT[b]).then_inc(s_xt[b % 2], 16)
                if b == 0:
                    for which in range(3):
                        sp.dma_start(w_raw[:, 0, which], WT[0, :, which]).then_inc(s_w[0], 16)
                if b < 2:
                    sp.dma_start(adj_tile[0][:, b], adj[b]).then_inc(s_adj[0][b], 16)
                if b == 0:
                    sp.dma_start(bias_all[:], bias.partition_broadcast(P)).then_inc(s_const, 16)
                    sp.dma_start(gain1[:], gain_cols).then_inc(s_const, 16)
                    sp.dma_start(shift1[:], shift_cols).then_inc(s_const, 16)
                    sp.dma_start(gain2[:], gain_row.partition_broadcast(P)).then_inc(s_const, 16)
                    sp.dma_start(shift2[:], shift_row.partition_broadcast(P)).then_inc(s_const, 16)
                if b == 1:
                    for which in range(3):
                        sp.dma_start(w_raw[:, 1, which], WT[1, :, which]).then_inc(s_w[1], 16)
            done(sp, s_diag[0], 0)
            sp.dma_start(adj_tile[0][:, 0], adj[2]).then_inc(s_adj[0][0], 16)

            def iteration(i, p):
                q = 1 - p
                if live(i, i + 3):
                    done(sp, s_lo[0], i + 1)
                    sp.dma_start(xt_raw[:, q], xT[i + 3]).then_inc(s_xt[q], 16)
                if live(i, i):
                    done(sp, s_attn[1], i - 2)
                    sp.dma_start(adj_tile[1][:, p], adj[i]).then_inc(s_adj[1][p], 16)
                if live(i, i - 2):
                    done(sp, s_y, i - 4)
                    sp.dma_start(xn[:, p], x[i - 2]).then_inc(s_xn[p], 16)
                if live(i, i + 3):
                    done(sp, s_attn[0], i + 1)
                    sp.dma_start(adj_tile[0][:, q], adj[i + 3]).then_inc(s_adj[0][q], 16)
                if live(i, i - 4):
                    done(sp, s_o, i - 4)
                    sp.dma_start(out[i - 4], o[:, p]).then_inc(s_out[p], 16)

            run(sp, iteration)
            moved(sp, s_out, G - 2, 0)
            moved(sp, s_out, G - 1, 1)

        @block.tensor
        def _(pe):
            def score_step(k, slot, n):
                c, (mv, st) = n // 3, TERMS[n % 3]
                return nc.tensor.matmul(p_score[k], hT[k][:, slot, st, c, :], hT[k][:, slot, mv, c, :],
                                        start=(n == 0), stop=(n == 8))

            def project_step(k, slot, which, n):
                c, (mv, st) = n // 3, TERMS[n % 3]
                return nc.tensor.matmul(p_proj[:, which, 0:D], hT[k][:, slot, st, c, :],
                                        w[:, k, which, mv, c, :], start=(n == 0), stop=(n == 8))

            def project_and_score(i, k, b, slot, b_other, slot_other, b_before):
                other = 1 - k
                project, score = live(i, b), live(i, b_other)
                if project:
                    before, b_last = (other, b_before) if live(i, b_before) else (k, b - 1)
                    done(pe, s_biased[before], b_last)
                    if isinstance(b, int) and b == 0:
                        pe.wait_ge(s_w_lo[k], LOW + 1)
                if score:
                    done(pe, s_lo[other], b_other)
                    done(pe, s_exp[other], b_other - 1)
                for n in range(18):
                    if project:
                        last = project_step(k, slot, UP + n // 9, n % 9)
                    if score and n % 2 == 0:
                        step = score_step(other, slot_other, n // 2)
                        if n == 16:
                            step.then_inc(s_score[other], 1)
                if project:
                    last.then_inc(s_proj[k], 1)
                    done(pe, s_attn[k], b)
                    done(pe, s_side[before], b_last)
                    done(pe, s_self_biased[before], b_last)
                    nc.tensor.transpose(p_attnT, A[k][:], ident[:]).then_inc(s_attnT[k], 1)
                    if isinstance(b, int) and b == 0:
                        pe.wait_ge(s_w_lo[k], SELF + 1)
                    for n in range(9):
                        last = project_step(k, slot, SELF, n)
                    last.then_inc(s_self[k], 1)

            def gather(k, b):
                done(pe, s_side_lo[k], b)
                done(pe, s_proj_lo[k], b)
                for side in (UP, LOW):
                    for n, (mv, st) in enumerate(TERMS):
                        last = nc.tensor.matmul(p_gather[k][:, 0:D], AT_split[k][:, st, side, :],
                                                proj_split[k][:, mv, side, :],
                                                start=(side == UP and n == 0), stop=(side == LOW and n == 2))
                last.then_inc(s_gather[k], 1)

            pe.wait_ge(s_setup, 5)
            project_and_score(-1, 1, -3, 1, 0, 0, -1)

            def iteration(i, p):
                q = 1 - p
                project_and_score(i, 0, i, p, i - 2, p, i - 3)
                if live(i, i - 3):
                    done(pe, s_whole[1], i - 4)
                    gather(1, i - 3)
                if live(i, i - 1):
                    done(pe, s_normed[0], i - 1)
                    for c in range(C):
                        last = nc.tensor.transpose(p_gather[0][:, c * P:(c + 1) * P],
                                                   normed[0][:, c * P:(c + 1) * P], ident[:])
                    last.then_inc(s_normedT, 1)
                project_and_score(i, 1, i - 2, p, i + 1, q, i)
                if live(i, i):
                    done(pe, s_relu, i - 1)
                    gather(0, i)

            run(pe, iteration)

        @block.vector
        def _(dve):
            def add_diagonal(k, b, slot):
                r = rows[k]
                done(dve, s_gather[k], b)
                done(dve, s_self_biased[k], b)
                done(dve, s_diag[k], b)
                done(dve, s_normed[k], b - 1)
                nc.vector.scalar_tensor_tensor(
                    out=gathered[k][:], in0=proj[k][:, SELF, :], scalar=col(r, slot, DIAG),
                    in1=p_gather[k][:, 0:D], op0=ALU.mult, op1=ALU.add).then_inc(s_whole[k], 1)
                done(dve, s_whole[k], b)
                nc.vector.bn_stats(stats6[k][:], gathered[k][:]).then_inc(s_stats[k], 1)
                own_wait(dve)
                done(dve, s_stats[k], b)
                nc.vector.bn_aggr(r[:, slot, MEAN:VAR + 1], stats6[k][:]).then_inc(s_moments[k], 1)
                done(dve, s_moments[k], b)
                done(dve, s_denom2[k], b)
                nc.vector.tensor_tensor(col(r, slot, VEPS), col(r, slot, VAR), col(r, slot, DENOM2),
                                        ALU.add).then_inc(s_veps[k], 1)

            def add_bias(k, b, sides_too):
                if sides_too:
                    done(dve, s_proj[k], b)
                    done(dve, s_proj_lo[k], b - 1)
                    nc.vector.tensor_tensor(proj[k][:, UP:LOW + 1, :], p_proj[:, UP:LOW + 1, 0:D],
                                            bias_all[:, k, UP:LOW + 1, :], ALU.add).then_inc(s_biased[k], 1)
                else:
                    done(dve, s_self[k], b)
                    done(dve, s_whole[k], b - 1)
                    nc.vector.tensor_tensor(proj[k][:, SELF, :], p_proj[:, SELF, 0:D],
                                            bias_all[:, k, SELF, :], ALU.add).then_inc(s_self_biased[k], 1)

            def row_max(k, b, slot):
                done(dve, s_score[k], b)
                nc.vector.reduce_max(col(rows[k], slot, ROWMAX), p_score[k], AX.X).then_inc(s_rowmax[k], 1)
                done(dve, s_rowmax[k], b)
                nc.vector.tensor_scalar(col(rows[k], slot, NEGMAX), col(rows[k], slot, ROWMAX), -SCALE, None,
                                        ALU.mult).then_inc(s_negmax[k], 1)

            def mask(k, b, slot):
                r = rows[k]
                done(dve, s_exp[k], b)
                moved(dve, s_adj[k], b, slot)
                done(dve, s_attnT[k], b - 1)
                nc.vector.tensor_tensor_reduce(A[k][:], E[k][:], adj_tile[k][:, slot, :], 1.0, 0.0, ALU.mult,
                                               ALU.add, col(r, slot, ADJSUM)).then_inc(s_attn[k], 1)
                done(dve, s_attn[k], b)
                nc.vector.tensor_tensor_reduce(diag_scratch[k][:], A[k][:], ident[:], 1.0, 0.0, ALU.mult,
                                               ALU.add, col(r, slot, DIAG)).then_inc(s_diag[k], 1)
                nc.vector.tensor_scalar(col(r, slot, DENOM), col(r, slot, EXPSUM), ATTN_EPS,
                                        col(r, slot, ADJSUM), ALU.mult, ALU.add).then_inc(s_denom[k], 1)
                done(dve, s_denom[k], b)
                nc.vector.scalar_tensor_tensor(
                    out=col(r, slot, DENOM2), in0=col(r, slot, DENOM), scalar=GNN_EPS,
                    in1=col(r, slot, DENOM), op0=ALU.mult, op1=ALU.mult).then_inc(s_denom2[k], 1)

            def cut_sides(k, b):
                done(dve, s_attnT[k], b)
                done(dve, s_side_lo[k], b - 1)
                nc.vector.tensor_tensor(AT[k][:], p_attnT.unsqueeze(1).broadcast_to([P, 2, N]), sides[:],
                                        ALU.mult).then_inc(s_side[k], 1)

            def residual(b, slot):
                done(dve, s_shifted, b)
                moved(dve, s_xn, b, slot)
                done(dve, s_o, b - 1)
                nc.vector.scalar_tensor_tensor(out=y[:], in0=shifted[:], scalar=0.0, in1=xn[:, slot, :],
                                               op0=ALU.max, op1=ALU.add).then_inc(s_y, 1)
                done(dve, s_y, b)
                nc.vector.bn_stats(y_stats6[:], y[:]).then_inc(s_y_stats, 1)
                own_wait(dve)
                done(dve, s_y_stats, b)
                nc.vector.bn_aggr(y_rows[:, slot, MEAN:VAR + 1], y_stats6[:]).then_inc(s_y_moments, 1)
                done(dve, s_y_moments, b)
                nc.vector.tensor_scalar(col(y_rows, slot, VEPS), col(y_rows, slot, VAR), OUT_EPS, None,
                                        ALU.add).then_inc(s_y_veps, 1)

            def low_weights(k):
                for which in range(3):
                    dve.wait_ge(s_w_hi[k], which + 1)
                    nc.vector.tensor_tensor(w[:, k, which, LO], w_raw[:, k, which],
                                            w[:, k, which, HI].bitcast(F32),
                                            ALU.subtract).then_inc(s_w_lo[k], 1)

            low_weights(0)
            row_max(0, 0, 0)
            dve.wait_ge(s_setup, 5)
            mask(0, 0, 0)
            dve.wait_ge(s_const, 80)

            def iteration(i, p):
                q = 1 - p
                if live(i, i - 1):
                    add_diagonal(0, i - 1, q)
                if live(i, i - 4):
                    residual(i - 4, p)
                if live(i, i):
                    add_bias(0, i, True)
                if live(i, i - 2):
                    row_max(1, i - 2, p)
                if live(i, i):
                    cut_sides(0, i)
                    add_bias(0, i, False)
                if live(i, i - 2):
                    mask(1, i - 2, p)
                if isinstance(i, int) and i == 0:
                    low_weights(1)
                if live(i, i - 3):
                    add_diagonal(1, i - 3, q)
                if live(i, i - 1):
                    done(dve, s_hi[1], i - 1)
                    done(dve, s_self[1], i - 3)
                    nc.vector.tensor_tensor(hT[1][:, q, LO], relu_T[:], hT[1][:, q, HI].bitcast(F32),
                                            ALU.subtract).then_inc(s_lo[1], 1)
                if live(i, i - 2):
                    add_bias(1, i - 2, True)
                if live(i, i + 1):
                    row_max(0, i + 1, q)
                if live(i, i - 2):
                    cut_sides(1, i - 2)
                    add_bias(1, i - 2, False)
                if live(i, i + 1):
                    mask(0, i + 1, q)

            run(dve, iteration)

        @block.scalar
        def _(act):
            def exponentials(k, b, slot):
                done(act, s_negmax[k], b)
                done(act, s_attn[k], b - 1)
                nc.scalar.activation(E[k][:], p_score[k], ACT.Exp, bias=col(rows[k], slot, NEGMAX),
                                     scale=SCALE, accum_out=col(rows[k], slot, EXPSUM)).then_inc(s_exp[k], 1)

            def high_sides(k, b):
                done(act, s_side[k], b)
                done(act, s_gather[k], b - 1)
                nc.scalar.activation(AT_split[k][:, HI], AT[k][:], ACT.Copy).then_inc(s_side_hi[k], 1)

            def high_projections(k, b):
                done(act, s_biased[k], b)
                done(act, s_gather[k], b - 1)
                nc.scalar.activation(proj_split[k][:, HI], proj[k][:, UP:LOW + 1, :],
                                     ACT.Copy).then_inc(s_proj_hi[k], 1)

            def normalise(k, b, slot):
                done(act, s_nbias[k], b)
                done(act, (s_normedT, s_scaled)[k], b - 1)
                nc.scalar.activation(normed[k][:], gathered[k][:], ACT.Identity,
                                     bias=col(rows[k], slot, NBIAS),
                                     scale=col(rows[k], slot, RSTD)).then_inc(s_normed[k], 1)

            def high_input(b, slot):
                moved(act, s_xt, b, slot)
                done(act, s_self[0], b - 2)
                nc.scalar.activation(hT[0][:, slot, HI], xt_raw[:, slot], ACT.Copy).then_inc(s_hi[0], 1)

            def high_weights(k):
                for which in range(3):
                    if which == 0:
                        act.wait_ge(s_w[k], 48)
                    nc.scalar.activation(w[:, k, which, HI], w_raw[:, k, which],
                                         ACT.Copy).then_inc(s_w_hi[k], 1)

            high_input(0, 0)
            high_weights(0)
            exponentials(0, 0, 0)
            act.wait_ge(s_const, 80)

            def iteration(i, p):
                q = 1 - p
                if live(i, i + 1):
                    high_input(i + 1, q)
                if live(i, i - 1):
                    normalise(0, i - 1, q)
                if live(i, i - 2):
                    exponentials(1, i - 2, p)
                if live(i, i):
                    high_sides(0, i)
                    high_projections(0, i)
                if isinstance(i, int) and i == 0:
                    high_weights(1)
                if live(i, i - 4):
                    done(act, s_y_nbias, i - 4)
                    moved(act, s_out, i - 6, p)
                    nc.scalar.activation(o[:, p, :], y[:], ACT.Identity, bias=col(y_rows, p, NBIAS),
                                         scale=col(y_rows, p, RSTD)).then_inc(s_o, 1)
                if live(i, i - 1):
                    done(act, s_normedT, i - 1)
                    done(act, s_lo[1], i - 2)
                    for c in range(C):
                        last = nc.scalar.activation(relu_T[:, c, :], p_gather[0][:, c * P:(c + 1) * P],
                                                    ACT.Relu, bias=shift1[:, c:c + 1],
                                                    scale=gain1[:, c:c + 1])
                    last.then_inc(s_relu, 1)
                    done(act, s_relu, i - 1)
                    done(act, s_self[1], i - 3)
                    nc.scalar.activation(hT[1][:, q, HI], relu_T[:], ACT.Copy).then_inc(s_hi[1], 1)
                if live(i, i - 3):
                    normalise(1, i - 3, q)
                if live(i, i + 1):
                    exponentials(0, i + 1, q)
                if live(i, i - 2):
                    high_sides(1, i - 2)
                    high_projections(1, i - 2)

            run(act, iteration)

        @block.gpsimd
        def _(pool):
            def low_sides(k, b):
                done(pool, s_side_hi[k], b)
                nc.gpsimd.tensor_tensor(AT_split[k][:, LO], AT[k][:], AT_split[k][:, HI].bitcast(F32),
                                        ALU.subtract).then_inc(s_side_lo[k], 1)

            def low_projections(k, b):
                done(pool, s_proj_hi[k], b)
                nc.gpsimd.tensor_tensor(proj_split[k][:, LO], proj[k][:, UP:LOW + 1, :],
                                        proj_split[k][:, HI].bitcast(F32),
                                        ALU.subtract).then_inc(s_proj_lo[k], 1)

            def deviation(r, b, slot, veps, rstd, nbias):
                done(pool, veps, b)
                nc.gpsimd.tensor_tensor(col(r, slot, RSTD), col(r, slot, VEPS), neg_half[:],
                                        ALU.pow).then_inc(rstd, 1)
                own_wait(pool)
                done(pool, rstd, b)
                nc.gpsimd.tensor_scalar(col(r, slot, NBIAS), col(r, slot, MEAN), col(r, slot, RSTD), -1.0,
                                        ALU.mult, ALU.mult).then_inc(nbias, 1)

            def low_input(b, slot):
                done(pool, s_hi[0], b)
                nc.gpsimd.tensor_tensor(hT[0][:, slot, LO], xt_raw[:, slot], hT[0][:, slot, HI].bitcast(F32),
                                        ALU.subtract).then_inc(s_lo[0], 1)

            nc.gpsimd.memset(ident[:], 0.0).then_inc(s_setup, 1)
            nc.gpsimd.memset(sides[:], 1.0).then_inc(s_setup, 1)
            nc.gpsimd.memset(neg_half[:], -0.5)
            pool.wait_ge(s_setup, 2)
            nc.gpsimd.affine_select(out=ident[:], in_=ident[:], compare_op=ALU.not_equal, fill=1.0, base=0,
                                    pattern=[[-1, P]], channel_multiplier=1).then_inc(s_setup, 1)
            nc.gpsimd.affine_select(out=sides[:, UP, :], in_=sides[:, UP, :], compare_op=ALU.is_gt, fill=0.0,
                                    base=0, pattern=[[-1, P]], channel_multiplier=1).then_inc(s_setup, 1)
            nc.gpsimd.affine_select(out=sides[:, LOW, :], in_=sides[:, LOW, :], compare_op=ALU.is_gt,
                                    fill=0.0, base=0, pattern=[[1, P]],
                                    channel_multiplier=-1).then_inc(s_setup, 1)
            pool.wait_ge(s_setup, 5)
            low_input(0, 0)

            def iteration(i, p):
                q = 1 - p
                if live(i, i - 3):
                    low_projections(1, i - 3)
                if live(i, i - 1):
                    deviation(rows[0], i - 1, q, s_veps[0], s_rstd[0], s_nbias[0])
                if live(i, i + 1):
                    low_input(i + 1, q)
                if live(i, i - 4):
                    deviation(y_rows, i - 4, p, s_y_veps, s_y_rstd, s_y_nbias)
                if live(i, i):
                    low_sides(0, i)
                    low_projections(0, i)
                if live(i, i - 3):
                    deviation(rows[1], i - 3, q, s_veps[1], s_rstd[1], s_nbias[1])
                    done(pool, s_normed[1], i - 3)
                    nc.gpsimd.tensor_tensor(scaled[:], normed[1][:], gain2[:], ALU.mult).then_inc(s_scaled, 1)
                    done(pool, s_scaled, i - 3)
                    done(pool, s_y, i - 4)
                    nc.gpsimd.tensor_tensor(shifted[:], scaled[:], shift2[:],
                                            ALU.add).then_inc(s_shifted, 1)
                if live(i, i - 2):
                    low_sides(1, i - 2)

            run(pool, iteration)


def kernel(x, adj, L0_gnn_Wl, L0_gnn_bl, L0_gnn_Ws, L0_gnn_bs, L0_gnn_Wr, L0_gnn_br, L0_gnn_ln_w, L0_gnn_ln_b):
    import numpy as np
    import concourse.bacc as bacc
    from concourse.bass_utils import run_bass_kernel_spmd

    G, N, D = x.shape
    C = D // P
    W = np.stack([L0_gnn_Wl, L0_gnn_Wr, L0_gnn_Ws], axis=1)
    W = W.reshape(2, 3, D, C, P).transpose(0, 4, 1, 3, 2)
    arrays = {
        "xT": np.asarray(x).reshape(G, N, C, P).transpose(0, 3, 2, 1),
        "x": x,
        "adj": adj,
        "WT": W,
        "bias": np.stack([L0_gnn_bl, L0_gnn_br, L0_gnn_bs], axis=1),
        "gain_cols": np.asarray(L0_gnn_ln_w)[0].reshape(C, P).T,
        "shift_cols": np.asarray(L0_gnn_ln_b)[0].reshape(C, P).T,
        "gain_row": np.asarray(L0_gnn_ln_w)[1],
        "shift_row": np.asarray(L0_gnn_ln_b)[1],
    }
    arrays = {name: np.ascontiguousarray(a) for name, a in arrays.items()}
    nc = bacc.Bacc("TRN2", target_bir_lowering=False, num_devices=1)
    args = [nc.dram_tensor(name, a.shape, mybir.dt.from_np(a.dtype), kind="ExternalInput").ap()
            for name, a in arrays.items()]
    args.append(nc.dram_tensor("out", (G, N, D), F32, kind="ExternalOutput").ap())
    graph_block(nc, *args)
    r = run_bass_kernel_spmd(nc, [arrays], core_ids=[0])
    return r.results[0]["out"]
```

```python
from contextlib import ExitStack

import concourse.bass as bass
from concourse import mybir

F32 = mybir.dt.float32
F32R = mybir.dt.float32r
ALU = mybir.AluOpType
ACT = mybir.ActivationFunctionType
AX = mybir.AxisListType

P = 128
UP, LOW, SELF = range(3)
HI, LO = range(2)
TERMS = [(HI, HI), (LO, HI), (HI, LO)]
NEGMAX, EXPSUM, ADJSUM, DENOM, DIAG, COLS = range(6)
LAYER, FINAL = range(2)

ATTN_EPS = 1e-10
GNN_EPS = 1e-12
OUT_EPS = 1e-5
MOST = 3.4e38


def graph_block(nc: bass.Bass, xT: bass.AP, x: bass.AP, adj: bass.AP, WT: bass.AP, bias: bass.AP,
                gain_cols: bass.AP, shift_cols: bass.AP, gain_row: bass.AP, shift_row: bass.AP, out: bass.AP):
    G, N, D = x.shape
    C = D // P
    assert N == P and D == C * P and G % 4 == 0 and G >= 12
    SCALE = float(D) ** -0.5
    FIRST, LAST = 4, G - 4
    UNROLL = 4
    END = G + 4

    with ExitStack() as ctx:
        def sb(name, shape, dtype=F32):
            return ctx.enter_context(nc.sbuf_tensor(name, shape, dtype))

        def bank(name, shape):
            return ctx.enter_context(nc.psum_tensor(name, shape, F32))

        def sem(name):
            return ctx.enter_context(nc.semaphore(name))

        w_raw = sb("w_raw", [P, 2, 3, C, D])
        w = sb("w", [P, 2, 3, 2, C, D], F32R)
        bias_all = sb("bias_all", [P, 2, 3, D])
        gain1 = sb("gain1", [P, C])
        shift1 = sb("shift1", [P, C])
        gain2 = sb("gain2", [P, D])
        shift2 = sb("shift2", [P, D])
        ident = sb("ident", [P, P])
        ident_r = sb("ident_r", [P, P], F32R)
        sides = sb("sides", [P, 2, P])
        neg_half = sb("neg_half", [P, 2])
        xt_raw = sb("xt_raw", [P, 2, C, N])
        xn = sb("xn", [P, 2, D])
        adj_tile = [sb("adj_layer1", [P, 2, N]), sb("adj_layer2", [P, 2, N])]
        hT = [sb("hT_layer1", [P, 2, 2, C, N], F32R), sb("hT_layer2", [P, 2, 2, C, N], F32R)]
        cross = [sb(f"cross{k}", [P, N], F32R) for k in (1, 2)]
        U = [sb(f"scores{k}", [P, N]) for k in (1, 2)]
        A = [sb(f"attn{k}", [P, N]) for k in (1, 2)]
        diag_scratch = [sb(f"diag_scratch{k}", [P, N]) for k in (1, 2)]
        AT = [sb(f"attnT{k}", [P, 2, N]) for k in (1, 2)]
        AT_split = [sb(f"attnT_split{k}", [P, 2, 2, N], F32R) for k in (1, 2)]
        proj = [sb(f"proj{k}", [P, 3, D]) for k in (1, 2)]
        proj_split = [sb(f"proj_split{k}", [P, 2, 2, D], F32R) for k in (1, 2)]
        gathered = [sb(f"gathered{k}", [P, D]) for k in (1, 2)]
        normed = [sb(f"normed{k}", [P, D]) for k in (1, 2)]
        stats6 = [sb(f"stats6_{k}", [P, 2, 6]) for k in (1, 2)]
        rows = [sb(f"rows{k}", [P, 2, COLS]) for k in (1, 2)]
        scaled = sb("scaled", [P, D])
        shifted = sb("shifted", [P, D])
        y = sb("y", [P, D])
        moments = [sb(f"moments{k}", [P, 2, 2]) for k in (1, 2)]
        neg_mean = [sb(f"neg_mean{k}", [P, 2]) for k in (1, 2)]
        eps_units = [sb(f"eps_units{k}", [P, 2, 2]) for k in (1, 2)]
        veps = [sb(f"veps{k}", [P, 2]) for k in (1, 2)]
        rstd = [sb(f"rstd{k}", [P, 2]) for k in (1, 2)]
        nbias = [sb(f"nbias{k}", [P, 2]) for k in (1, 2)]
        o = sb("o", [P, 2, D])

        p_proj = bank("p_proj", [P, 3, 512])
        p_gather = [bank("p_gather1", [P, 512]), bank("p_gather2", [P, 512])]
        p_score = [bank("p_score1", [P, 4, N]), bank("p_score2", [P, 4, N])]
        E = [p_score[0][:, 2, :], p_score[1][:, 2, :]]
        p_attnT = bank("p_attnT", [P, 512])[:, 0:N]

        relu_T = p_gather[0][:, 0:D].rearrange("p (c n) -> p c n", c=C)

        s_w = [[sem(f"s_w{k}_{name}") for name in ("up", "low", "self")] for k in (1, 2)]
        s_const = sem("s_const")
        s_xt = [sem("s_xt_even"), sem("s_xt_odd")]
        s_xn = [sem("s_xn_even"), sem("s_xn_odd")]
        s_adj = [[sem("s_adj1_even"), sem("s_adj1_odd")], [sem("s_adj2_even"), sem("s_adj2_odd")]]
        s_out = [sem("s_out_even"), sem("s_out_odd")]
        s_setup = sem("s_setup")
        s_ident_r = sem("s_ident_r")
        s_eps = sem("s_eps")
        s_w_hi = [sem("s_w_hi1"), sem("s_w_hi2")]
        s_w_lo = [sem("s_w_lo1"), sem("s_w_lo2")]

        def per_layer(name):
            return [sem(f"{name}1"), sem(f"{name}2")]

        s_hi = per_layer("s_hi")
        s_lo = per_layer("s_lo")
        s_parts = per_layer("s_parts")
        s_score = per_layer("s_score")
        s_cross = per_layer("s_cross")
        s_negmax = per_layer("s_negmax")
        s_exp = per_layer("s_exp")
        s_attn = per_layer("s_attn")
        s_diag = per_layer("s_diag")
        s_denom = per_layer("s_denom")
        s_denom2 = per_layer("s_denom2")
        s_attnT = per_layer("s_attnT")
        s_side = per_layer("s_side")
        s_side_hi = per_layer("s_side_hi")
        s_side_lo = per_layer("s_side_lo")
        s_proj = per_layer("s_proj")
        s_self = per_layer("s_self")
        s_biased = per_layer("s_biased")
        s_self_biased = per_layer("s_self_biased")
        s_proj_hi = per_layer("s_proj_hi")
        s_proj_lo = per_layer("s_proj_lo")
        s_gather = per_layer("s_gather")
        s_whole = per_layer("s_whole")
        s_stats = per_layer("s_stats")
        s_moments = per_layer("s_moments")
        s_veps = per_layer("s_veps")
        s_rstd = per_layer("s_rstd")
        s_nbias = per_layer("s_nbias")
        s_normed = per_layer("s_normed")
        s_normedT = sem("s_normedT")
        s_relu = sem("s_relu")
        s_scaled = sem("s_scaled")
        s_shifted = sem("s_shifted")
        s_y = sem("s_y")
        s_y_stats = sem("s_y_stats")
        s_y_moments = sem("s_y_moments")
        s_y_rstd = sem("s_y_rstd")
        s_y_nbias = sem("s_y_nbias")
        s_y_only = sem("s_y_only")
        s_o = sem("s_o")

        def live(i, b):
            return not isinstance(i, int) or 0 <= b < G

        def done(eng, s, b):
            if not isinstance(b, int) or b >= 0:
                eng.wait_ge(s, b + 1)

        def moved(eng, pair, b, slot):
            if not isinstance(b, int) or b >= 0:
                eng.wait_ge(pair[slot], (b - slot) * 8 + 16)

        def done_apart(eng, s, b):
            count = b + 1 if isinstance(b, int) else eng.snap(b + 1)
            eng.wait_ge(s_setup, 5)
            eng.wait_ge(s, count)

        def run(eng, iteration):
            for i in range(FIRST):
                iteration(i, i % 2)
            with eng.Fori(FIRST, LAST - UNROLL + 1, UNROLL) as i:
                for n in range(UNROLL):
                    iteration(i + n, n % 2)
            for i in range(LAST, END):
                iteration(i, i % 2)

        def col(tile, slot, k):
            return tile[:, slot, k:k + 1]

        block = ctx.enter_context(nc.Block())

        @block.sync
        def _(sp):
            for b in (0, 1, 2):
                if b == 2:
                    done(sp, s_lo[0], 0)
                sp.dma_start(xt_raw[:, b % 2], xT[b]).then_inc(s_xt[b % 2], 16)
                if b == 0:
                    for which in range(3):
                        sp.dma_start(w_raw[:, 0, which], WT[0, :, which]).then_inc(s_w[0][which], 16)
                if b < 2:
                    sp.dma_start(adj_tile[0][:, b], adj[b]).then_inc(s_adj[0][b], 16)
                if b == 0:
                    sp.dma_start(bias_all[:], bias.partition_broadcast(P)).then_inc(s_const, 16)
                    sp.dma_start(gain1[:], gain_cols).then_inc(s_const, 16)
                    sp.dma_start(shift1[:], shift_cols).then_inc(s_const, 16)
                    sp.dma_start(gain2[:], gain_row.partition_broadcast(P)).then_inc(s_const, 16)
                    sp.dma_start(shift2[:], shift_row.partition_broadcast(P)).then_inc(s_const, 16)
                if b == 1:
                    for which in range(3):
                        sp.dma_start(w_raw[:, 1, which], WT[1, :, which]).then_inc(s_w[1][which], 16)
            done(sp, s_diag[0], 0)
            sp.dma_start(adj_tile[0][:, 0], adj[2]).then_inc(s_adj[0][0], 16)

            def iteration(i, p):
                q = 1 - p
                if live(i, i + 3):
                    done(sp, s_lo[0], i + 1)
                    sp.dma_start(xt_raw[:, q], xT[i + 3]).then_inc(s_xt[q], 16)
                if live(i, i):
                    done(sp, s_attn[1], i - 2)
                    sp.dma_start(adj_tile[1][:, p], adj[i]).then_inc(s_adj[1][p], 16)
                if live(i, i - 2):
                    done(sp, s_y, i - 4)
                    sp.dma_start(xn[:, p], x[i - 2]).then_inc(s_xn[p], 16)
                if live(i, i + 3):
                    done(sp, s_attn[0], i + 1)
                    sp.dma_start(adj_tile[0][:, q], adj[i + 3]).then_inc(s_adj[0][q], 16)
                if live(i, i - 4):
                    done(sp, s_o, i - 4)
                    sp.dma_start(out[i - 4], o[:, p]).then_inc(s_out[p], 16)

            run(sp, iteration)
            moved(sp, s_out, G - 2, 0)
            moved(sp, s_out, G - 1, 1)

        @block.tensor
        def _(pe):
            def score_step(k, slot, n):
                return nc.tensor.matmul(p_score[k][:, HI:LO + 1, :], hT[k][:, slot, HI, n, :],
                                        hT[k][:, slot, HI:LO + 1, n, :], start=(n == 0), stop=(n == C - 1))

            def project_step(k, slot, which, n):
                c, (mv, st) = n // 3, TERMS[n % 3]
                return nc.tensor.matmul(p_proj[:, which, 0:D], hT[k][:, slot, st, c, :],
                                        w[:, k, which, mv, c, :], start=(n == 0), stop=(n == 8))

            def project_and_score(i, k, b, slot, b_other, slot_other, b_before):
                other = 1 - k
                project, score = live(i, b), live(i, b_other)
                if project:
                    before, b_last = (other, b_before) if live(i, b_before) else (k, b - 1)
                    done(pe, s_biased[before], b_last)
                if score:
                    done(pe, s_lo[other], b_other)
                for n in range(18):
                    if project:
                        if isinstance(b, int) and b == 0 and n % 9 == 0:
                            pe.wait_ge(s_w_lo[k], UP + n // 9 + 1)
                        last = project_step(k, slot, UP + n // 9, n % 9)
                    if score and n % 2 == 0 and n // 2 < C:
                        step = score_step(other, slot_other, n // 2)
                        if n // 2 == C - 1:
                            step.then_inc(s_parts[other], 1)
                    if score and n == 14:
                        done(pe, s_cross[other], b_other)
                        nc.tensor.matmul(p_score[other][:, HI, :], cross[other][:], ident_r[:], start=False,
                                         stop=True, skip_group_check=True).then_inc(s_score[other], 1)
                if project:
                    last.then_inc(s_proj[k], 1)
                    done(pe, s_attn[k], b)
                    nc.tensor.transpose(p_attnT, A[k][:], ident[:]).then_inc(s_attnT[k], 1)
                    if isinstance(b, int) and b == 0:
                        pe.wait_ge(s_w_lo[k], SELF + 1)
                    for n in range(9):
                        last = project_step(k, slot, SELF, n)
                    last.then_inc(s_self[k], 1)

            def gather(k, b):
                done(pe, s_side_lo[k], b)
                done(pe, s_proj_lo[k], b)
                for side in (UP, LOW):
                    for n, (mv, st) in enumerate(TERMS):
                        last = nc.tensor.matmul(p_gather[k][:, 0:D], AT_split[k][:, st, side, :],
                                                proj_split[k][:, mv, side, :],
                                                start=(side == UP and n == 0), stop=(side == LOW and n == 2))
                last.then_inc(s_gather[k], 1)

            pe.wait_ge(s_setup, 5)
            pe.wait_ge(s_ident_r, 1)
            project_and_score(-1, 1, -3, 1, 0, 0, -1)

            def iteration(i, p):
                q = 1 - p
                project_and_score(i, 0, i, p, i - 2, p, i - 3)
                if live(i, i - 3):
                    gather(1, i - 3)
                if live(i, i - 1):
                    done(pe, s_normed[0], i - 1)
                    for c in range(C):
                        last = nc.tensor.transpose(p_gather[0][:, c * P:(c + 1) * P],
                                                   normed[0][:, c * P:(c + 1) * P], ident[:])
                    last.then_inc(s_normedT, 1)
                project_and_score(i, 1, i - 2, p, i + 1, q, i)
                if live(i, i):
                    done(pe, s_lo[1], i - 1)
                    gather(0, i)

            run(pe, iteration)

        @block.vector
        def _(dve):
            def normalise_rows(k, b, slot, b_y, slot_y):
                layer, final = b is not None, b_y is not None
                if layer:
                    done(dve, s_gather[k], b)
                    done(dve, s_diag[k], b)
                    if k == 1:
                        done(dve, s_normed[k], b - 1)
                    nc.vector.scalar_tensor_tensor(
                        out=gathered[k][:], in0=proj[k][:, SELF, :], scalar=col(rows[k], slot, DIAG),
                        in1=p_gather[k][:, 0:D], op0=ALU.mult, op1=ALU.add).then_inc(s_whole[k], 1)
                if final:
                    done(dve, s_shifted, b_y)
                    moved(dve, s_xn, b_y, slot_y)
                    done(dve, s_o, b_y - 1)
                    nc.vector.scalar_tensor_tensor(out=y[:], in0=shifted[:], scalar=0.0,
                                                   in1=xn[:, slot_y, :], op0=ALU.max,
                                                   op1=ALU.add).then_inc(s_y, 1)
                if layer:
                    done(dve, s_whole[k], b)
                    nc.vector.bn_stats(stats6[k][:, LAYER], gathered[k][:]).then_inc(s_stats[k], 1)
                if final:
                    done(dve, s_y, b_y)
                    nc.vector.bn_stats(stats6[k][:, FINAL], y[:]).then_inc(s_y_stats, 1)
                if layer:
                    done_apart(dve, s_stats[k], b)
                    nc.vector.bn_aggr(moments[k][:, LAYER], stats6[k][:, LAYER]).then_inc(s_moments[k], 1)
                if final:
                    done_apart(dve, s_y_stats, b_y)
                    nc.vector.bn_aggr(moments[k][:, FINAL], stats6[k][:, FINAL]).then_inc(s_y_moments, 1)
                which = slice(FINAL if not layer else LAYER, FINAL + 1 if final else LAYER + 1)
                last = s_y_only if not layer else s_veps[k]
                if layer:
                    done(dve, s_moments[k], b)
                    done(dve, s_denom2[k], b)
                if final:
                    done(dve, s_y_moments, b_y)
                nc.vector.scalar_tensor_tensor(
                    out=veps[k][:, which], in0=eps_units[k][:, slot, which], scalar=GNN_EPS,
                    in1=moments[k][:, which, 1], op0=ALU.mult, op1=ALU.add)
                nc.vector.tensor_scalar(neg_mean[k][:, which], moments[k][:, which, 0], -1.0, None,
                                        ALU.mult).then_inc(last, 1)

            def add_bias(k, b, sides_too):
                if sides_too:
                    done(dve, s_proj[k], b)
                    nc.vector.tensor_tensor(proj[k][:, UP:LOW + 1, :], p_proj[:, UP:LOW + 1, 0:D],
                                            bias_all[:, k, UP:LOW + 1, :], ALU.add).then_inc(s_biased[k], 1)
                else:
                    done(dve, s_self[k], b)
                    nc.vector.tensor_tensor(proj[k][:, SELF, :], p_proj[:, SELF, 0:D],
                                            bias_all[:, k, SELF, :], ALU.add).then_inc(s_self_biased[k], 1)

            def scaled_scores(k, b, slot):
                nc.vector.tensor_tensor_reduce(U[k][:], p_score[k][:, HI, :], cross[k][:].bitcast(F32), -SCALE,
                                               MOST, ALU.add, ALU.min, col(rows[k], slot, NEGMAX)).then_inc(s_negmax[k], 1)

            def mask(k, b, slot):
                done(dve, s_exp[k], b)
                moved(dve, s_adj[k], b, slot)
                nc.vector.tensor_tensor_reduce(A[k][:], E[k], adj_tile[k][:, slot, :], 1.0, 0.0, ALU.mult,
                                               ALU.add, col(rows[k], slot, ADJSUM)).then_inc(s_attn[k], 1)

            def cut_sides(k, b, slot):
                done(dve, s_attnT[k], b)
                nc.vector.tensor_tensor(AT[k][:], p_attnT.unsqueeze(1).broadcast_to([P, 2, N]), sides[:],
                                        ALU.mult).then_inc(s_side[k], 1)
                nc.vector.tensor_tensor_reduce(diag_scratch[k][:], p_attnT, ident[:], 1.0, 0.0, ALU.mult,
                                               ALU.add, col(rows[k], slot, DIAG)).then_inc(s_diag[k], 1)

            def low_weights(k):
                for which in range(3):
                    dve.wait_ge(s_w_hi[k], which + 1)
                    nc.vector.tensor_tensor(w[:, k, which, LO], w_raw[:, k, which],
                                            w[:, k, which, HI].bitcast(F32),
                                            ALU.subtract).then_inc(s_w_lo[k], 1)

            dve.wait_ge(s_setup, 5)
            nc.vector.tensor_copy(ident_r[:], ident[:]).then_inc(s_ident_r, 1)
            for k in (0, 1):
                nc.vector.memset(eps_units[k][:], OUT_EPS / GNN_EPS).then_inc(s_eps, 1)
            low_weights(0)
            done(dve, s_score[0], 0)
            scaled_scores(0, 0, 0)
            mask(0, 0, 0)
            dve.wait_ge(s_const, 80)

            def iteration(i, p):
                q = 1 - p
                if live(i, i - 1) or live(i, i - 4):
                    normalise_rows(0, i - 1 if live(i, i - 1) else None, q,
                                   i - 4 if live(i, i - 4) else None, p)
                if live(i, i):
                    add_bias(0, i, True)
                if live(i, i - 2):
                    done(dve, s_score[1], i - 2)
                if live(i, i):
                    cut_sides(0, i, p)
                if live(i, i - 2):
                    scaled_scores(1, i - 2, p)
                if live(i, i):
                    add_bias(0, i, False)
                if live(i, i - 2):
                    mask(1, i - 2, p)
                if isinstance(i, int) and i == 0:
                    low_weights(1)
                if live(i, i - 3):
                    normalise_rows(1, i - 3, q, None, 0)
                if live(i, i - 1):
                    done(dve, s_hi[1], i - 1)
                    nc.vector.tensor_tensor(hT[1][:, q, LO], relu_T, hT[1][:, q, HI].bitcast(F32),
                                            ALU.subtract).then_inc(s_lo[1], 1)
                if live(i, i - 2):
                    add_bias(1, i - 2, True)
                if live(i, i + 1):
                    done(dve, s_score[0], i + 1)
                if live(i, i - 2):
                    cut_sides(1, i - 2, p)
                if live(i, i + 1):
                    scaled_scores(0, i + 1, q)
                if live(i, i - 2):
                    add_bias(1, i - 2, False)
                if live(i, i + 1):
                    mask(0, i + 1, q)

            run(dve, iteration)

        @block.scalar
        def _(act):
            def cross_scores(k, b):
                done(act, s_parts[k], b)
                nc.scalar.activation(cross[k][:], p_score[k][:, LO, :], ACT.Copy).then_inc(s_cross[k], 1)

            def exponentials(k, b, slot):
                done(act, s_negmax[k], b)
                nc.scalar.activation(E[k], U[k][:], ACT.Exp, bias=col(rows[k], slot, NEGMAX),
                                     scale=-1.0, accum_out=col(rows[k], slot, EXPSUM)).then_inc(s_exp[k], 1)

            def high_sides(k, b):
                done(act, s_side[k], b)
                nc.scalar.activation(AT_split[k][:, HI], AT[k][:], ACT.Copy).then_inc(s_side_hi[k], 1)

            def high_projections(k, b):
                done(act, s_biased[k], b)
                nc.scalar.activation(proj_split[k][:, HI], proj[k][:, UP:LOW + 1, :],
                                     ACT.Copy).then_inc(s_proj_hi[k], 1)

            def normalise(k, b, count, which, rows_in, rows_out, s_rows):
                done(act, count, b)
                nc.scalar.activation(rows_out, rows_in, ACT.Identity, bias=nbias[k][:, which:which + 1],
                                     scale=rstd[k][:, which:which + 1]).then_inc(s_rows, 1)

            def high_input(b, slot):
                moved(act, s_xt, b, slot)
                done(act, s_self[0], b - 2)
                nc.scalar.activation(hT[0][:, slot, HI], xt_raw[:, slot], ACT.Copy).then_inc(s_hi[0], 1)

            def high_weights(k):
                for which in range(3):
                    act.wait_ge(s_w[k][which], 16)
                    nc.scalar.activation(w[:, k, which, HI], w_raw[:, k, which],
                                         ACT.Copy).then_inc(s_w_hi[k], 1)

            high_input(0, 0)
            high_weights(0)
            cross_scores(0, 0)
            exponentials(0, 0, 0)
            act.wait_ge(s_const, 80)

            def iteration(i, p):
                q = 1 - p
                if live(i, i + 1):
                    high_input(i + 1, q)
                if live(i, i - 2):
                    cross_scores(1, i - 2)
                if live(i, i - 1):
                    normalise(0, i - 1, s_nbias[0], LAYER, gathered[0][:], normed[0][:], s_normed[0])
                if live(i, i):
                    high_sides(0, i)
                if live(i, i - 2):
                    exponentials(1, i - 2, p)
                if live(i, i):
                    high_projections(0, i)
                if isinstance(i, int) and i == 0:
                    high_weights(1)
                if live(i, i - 4):
                    moved(act, s_out, i - 6, p)
                    beside = live(i, i - 1)
                    normalise(0, i - 1 if beside else i - G - 1, s_nbias[0] if beside else s_y_nbias, FINAL,
                              y[:], o[:, p, :], s_o)
                if live(i, i + 1):
                    cross_scores(0, i + 1)
                if live(i, i - 1):
                    done(act, s_normedT, i - 1)
                    for c in range(C):
                        last = nc.scalar.activation(relu_T[:, c, :], relu_T[:, c, :], ACT.Relu,
                                                    bias=shift1[:, c:c + 1], scale=gain1[:, c:c + 1])
                    last.then_inc(s_relu, 1)
                    done(act, s_relu, i - 1)
                    done(act, s_self[1], i - 3)
                    nc.scalar.activation(hT[1][:, q, HI], relu_T, ACT.Copy).then_inc(s_hi[1], 1)
                if live(i, i - 3):
                    normalise(1, i - 3, s_nbias[1], LAYER, gathered[1][:], normed[1][:], s_normed[1])
                if live(i, i - 2):
                    high_sides(1, i - 2)
                if live(i, i + 1):
                    exponentials(0, i + 1, q)
                if live(i, i - 2):
                    high_projections(1, i - 2)

            run(act, iteration)

        @block.gpsimd
        def _(pool):
            def low_sides(k, b):
                done(pool, s_side_hi[k], b)
                nc.gpsimd.tensor_tensor(AT_split[k][:, LO], AT[k][:], AT_split[k][:, HI].bitcast(F32),
                                        ALU.subtract).then_inc(s_side_lo[k], 1)

            def low_projections(k, b):
                done(pool, s_proj_hi[k], b)
                nc.gpsimd.tensor_tensor(proj_split[k][:, LO], proj[k][:, UP:LOW + 1, :],
                                        proj_split[k][:, HI].bitcast(F32),
                                        ALU.subtract).then_inc(s_proj_lo[k], 1)

            def deviation(k, b, which, s_v, s_r, s_n):
                done(pool, s_v, b)
                nc.gpsimd.tensor_tensor(rstd[k][:, which], veps[k][:, which], neg_half[:, which],
                                        ALU.pow).then_inc(s_r, 1)
                done(pool, s_r, b)
                nc.gpsimd.tensor_tensor(nbias[k][:, which], neg_mean[k][:, which], rstd[k][:, which],
                                        ALU.mult).then_inc(s_n, 1)

            def denominator(k, b, slot):
                r = rows[k]
                nc.gpsimd.tensor_scalar(col(r, slot, DENOM), col(r, slot, EXPSUM), ATTN_EPS,
                                        col(r, slot, ADJSUM), ALU.mult, ALU.add).then_inc(s_denom[k], 1)
                done(pool, s_denom[k], b)
                nc.gpsimd.tensor_tensor(eps_units[k][:, slot, LAYER:LAYER + 1], col(r, slot, DENOM),
                                        col(r, slot, DENOM), ALU.mult).then_inc(s_denom2[k], 1)

            def low_input(b, slot):
                done(pool, s_hi[0], b)
                nc.gpsimd.tensor_tensor(hT[0][:, slot, LO], xt_raw[:, slot], hT[0][:, slot, HI].bitcast(F32),
                                        ALU.subtract).then_inc(s_lo[0], 1)

            nc.gpsimd.memset(ident[:], 0.0).then_inc(s_setup, 1)
            nc.gpsimd.memset(sides[:], 1.0).then_inc(s_setup, 1)
            nc.gpsimd.memset(neg_half[:], -0.5)
            pool.wait_ge(s_setup, 2)
            nc.gpsimd.affine_select(out=ident[:], in_=ident[:], compare_op=ALU.not_equal, fill=1.0, base=0,
                                    pattern=[[-1, P]], channel_multiplier=1).then_inc(s_setup, 1)
            nc.gpsimd.affine_select(out=sides[:, UP, :], in_=sides[:, UP, :], compare_op=ALU.is_gt, fill=0.0,
                                    base=0, pattern=[[-1, P]], channel_multiplier=1).then_inc(s_setup, 1)
            nc.gpsimd.affine_select(out=sides[:, LOW, :], in_=sides[:, LOW, :], compare_op=ALU.is_gt,
                                    fill=0.0, base=0, pattern=[[1, P]],
                                    channel_multiplier=-1).then_inc(s_setup, 1)
            pool.wait_ge(s_setup, 5)
            low_input(0, 0)
            pool.wait_ge(s_eps, 2)
            done(pool, s_attn[0], 0)
            denominator(0, 0, 0)

            def iteration(i, p):
                q = 1 - p
                if live(i, i - 3):
                    low_projections(1, i - 3)
                if live(i, i - 1):
                    deviation(0, i - 1, slice(LAYER, FINAL + 1 if live(i, i - 4) else LAYER + 1), s_veps[0],
                              s_rstd[0], s_nbias[0])
                elif live(i, i - 4):
                    deviation(0, i - G - 1, slice(FINAL, FINAL + 1), s_y_only, s_y_rstd, s_y_nbias)
                if live(i, i + 1):
                    low_input(i + 1, q)
                if live(i, i - 2):
                    done(pool, s_attn[1], i - 2)
                if live(i, i):
                    low_sides(0, i)
                if live(i, i - 2):
                    denominator(1, i - 2, p)
                if live(i, i):
                    low_projections(0, i)
                if live(i, i - 3):
                    deviation(1, i - 3, slice(LAYER, LAYER + 1), s_veps[1], s_rstd[1], s_nbias[1])
                    done(pool, s_normed[1], i - 3)
                    nc.gpsimd.tensor_tensor(scaled[:], normed[1][:], gain2[:], ALU.mult).then_inc(s_scaled, 1)
                    done(pool, s_scaled, i - 3)
                    done(pool, s_y, i - 4)
                    nc.gpsimd.tensor_tensor(shifted[:], scaled[:], shift2[:],
                                            ALU.add).then_inc(s_shifted, 1)
                if live(i, i + 1):
                    done(pool, s_attn[0], i + 1)
                if live(i, i - 2):
                    low_sides(1, i - 2)
                if live(i, i + 1):
                    denominator(0, i + 1, q)

            run(pool, iteration)


def kernel(x, adj, L0_gnn_Wl, L0_gnn_bl, L0_gnn_Ws, L0_gnn_bs, L0_gnn_Wr, L0_gnn_br, L0_gnn_ln_w, L0_gnn_ln_b):
    import numpy as np
    import concourse.bacc as bacc
    from concourse.bass_utils import run_bass_kernel_spmd

    G, N, D = x.shape
    C = D // P
    W = np.stack([L0_gnn_Wl, L0_gnn_Wr, L0_gnn_Ws], axis=1)
    W = W.reshape(2, 3, D, C, P).transpose(0, 4, 1, 3, 2)
    arrays = {
        "xT": np.asarray(x).reshape(G, N, C, P).transpose(0, 3, 2, 1),
        "x": x,
        "adj": adj,
        "WT": W,
        "bias": np.stack([L0_gnn_bl, L0_gnn_br, L0_gnn_bs], axis=1),
        "gain_cols": np.asarray(L0_gnn_ln_w)[0].reshape(C, P).T,
        "shift_cols": np.asarray(L0_gnn_ln_b)[0].reshape(C, P).T,
        "gain_row": np.asarray(L0_gnn_ln_w)[1],
        "shift_row": np.asarray(L0_gnn_ln_b)[1],
    }
    arrays = {name: np.ascontiguousarray(a) for name, a in arrays.items()}
    nc = bacc.Bacc("TRN2", target_bir_lowering=False, num_devices=1)
    args = [nc.dram_tensor(name, a.shape, mybir.dt.from_np(a.dtype), kind="ExternalInput").ap()
            for name, a in arrays.items()]
    args.append(nc.dram_tensor("out", (G, N, D), F32, kind="ExternalOutput").ap())
    graph_block(nc, *args)
    r = run_bass_kernel_spmd(nc, [arrays], core_ids=[0])
    return r.results[0]["out"]
```

```python
from contextlib import ExitStack

import concourse.bass as bass
from concourse import mybir

F32 = mybir.dt.float32
F32R = mybir.dt.float32r
ALU = mybir.AluOpType
ACT = mybir.ActivationFunctionType
AX = mybir.AxisListType

P = 128
UP, LOW, SELF = range(3)
HI, LO = range(2)
TERMS = [(HI, HI), (LO, HI), (HI, LO)]
NEGMAX, EXPSUM, ADJSUM, DENOM, DIAG, COLS = range(6)
LAYER, FINAL = range(2)

ATTN_EPS = 1e-10
GNN_EPS = 1e-12
OUT_EPS = 1e-5
MOST = 3.4e38


def graph_block(nc: bass.Bass, xT: bass.AP, x: bass.AP, adj: bass.AP, WT: bass.AP, bias: bass.AP,
                gain_cols: bass.AP, shift_cols: bass.AP, gain_row: bass.AP, shift_row: bass.AP, out: bass.AP):
    G, N, D = x.shape
    C = D // P
    assert N == P and D == C * P and G % 4 == 0 and G >= 12
    SCALE = float(D) ** -0.5
    FIRST, LAST = 4, G - 4
    UNROLL = 4
    END = G + 4

    with ExitStack() as ctx:
        def sb(name, shape, dtype=F32):
            return ctx.enter_context(nc.sbuf_tensor(name, shape, dtype))

        def bank(name, shape):
            return ctx.enter_context(nc.psum_tensor(name, shape, F32))

        def sem(name):
            return ctx.enter_context(nc.semaphore(name))

        w_raw = sb("w_raw", [P, 2, 3, C, D])
        w = sb("w", [P, 2, 3, 2, C, D], F32R)
        bias_all = sb("bias_all", [P, 2, 3, D])
        gain1 = sb("gain1", [P, C])
        shift1 = sb("shift1", [P, C])
        gain2 = sb("gain2", [P, D])
        shift2 = sb("shift2", [P, D])
        ident = sb("ident", [P, P])
        ident_r = sb("ident_r", [P, P], F32R)
        sides = sb("sides", [P, 2, P])
        neg_half = sb("neg_half", [P, 2])
        xt_raw = sb("xt_raw", [P, 2, C, N])
        xn = sb("xn", [P, 2, D])
        adj_tile = [sb("adj_layer1", [P, 2, N]), sb("adj_layer2", [P, 2, N])]
        hT = [sb("hT_layer1", [P, 2, 2, C, N], F32R), sb("hT_layer2", [P, 2, 2, C, N], F32R)]
        cross = [sb(f"cross{k}", [P, N], F32R) for k in (1, 2)]
        U = [sb(f"scores{k}", [P, N]) for k in (1, 2)]
        A = [sb(f"attn{k}", [P, N]) for k in (1, 2)]
        diag_scratch = [sb(f"diag_scratch{k}", [P, N]) for k in (1, 2)]
        AT = [sb(f"attnT{k}", [P, 2, N]) for k in (1, 2)]
        AT_split = [sb(f"attnT_split{k}", [P, 2, 2, N], F32R) for k in (1, 2)]
        proj = [sb(f"proj{k}", [P, 3, D]) for k in (1, 2)]
        proj_split = [sb(f"proj_split{k}", [P, 2, 2, D], F32R) for k in (1, 2)]
        gathered = [sb(f"gathered{k}", [P, D]) for k in (1, 2)]
        normed = [sb(f"normed{k}", [P, D]) for k in (1, 2)]
        stats6 = [sb(f"stats6_{k}", [P, 2, 6]) for k in (1, 2)]
        rows = [sb(f"rows{k}", [P, 2, COLS]) for k in (1, 2)]
        scaled = sb("scaled", [P, D])
        shifted = sb("shifted", [P, D])
        y = sb("y", [P, D])
        moments = [sb(f"moments{k}", [P, 2, 2]) for k in (1, 2)]
        neg_mean = [sb(f"neg_mean{k}", [P, 2]) for k in (1, 2)]
        eps_units = [sb(f"eps_units{k}", [P, 2, 2]) for k in (1, 2)]
        veps = [sb(f"veps{k}", [P, 2]) for k in (1, 2)]
        rstd = [sb(f"rstd{k}", [P, 2]) for k in (1, 2)]
        nbias = [sb(f"nbias{k}", [P, 2]) for k in (1, 2)]
        o = sb("o", [P, 2, D])

        p_proj = bank("p_proj", [P, 3, 512])
        p_gather = [bank("p_gather1", [P, 512]), bank("p_gather2", [P, 512])]
        p_score = [bank("p_score1", [P, 4, N]), bank("p_score2", [P, 4, N])]
        E = [p_score[0][:, 2, :], p_score[1][:, 2, :]]
        p_attnT = bank("p_attnT", [P, 512])[:, 0:N]

        relu_T = p_gather[0][:, 0:D].rearrange("p (c n) -> p c n", c=C)

        s_w = [[sem(f"s_w{k}_{name}") for name in ("up", "low", "self")] for k in (1, 2)]
        s_bias = [sem("s_bias1"), sem("s_bias2")]
        s_const = sem("s_const")
        s_xt = [sem("s_xt_even"), sem("s_xt_odd")]
        s_xn = [sem("s_xn_even"), sem("s_xn_odd")]
        s_adj = [[sem("s_adj1_even"), sem("s_adj1_odd")], [sem("s_adj2_even"), sem("s_adj2_odd")]]
        s_out = [sem("s_out_even"), sem("s_out_odd")]
        s_setup = sem("s_setup")
        s_ident_r = sem("s_ident_r")
        s_eps = sem("s_eps")
        s_w_hi = [[sem(f"s_w_hi{k}_{name}") for name in ("up", "low", "self")] for k in (1, 2)]
        s_w_lo = [sem("s_w_lo1"), sem("s_w_lo2")]

        def per_layer(name):
            return [sem(f"{name}1"), sem(f"{name}2")]

        s_hi = per_layer("s_hi")
        s_lo = per_layer("s_lo")
        s_parts = per_layer("s_parts")
        s_score = per_layer("s_score")
        s_cross = per_layer("s_cross")
        s_negmax = per_layer("s_negmax")
        s_exp = per_layer("s_exp")
        s_attn = per_layer("s_attn")
        s_diag = per_layer("s_diag")
        s_denom = per_layer("s_denom")
        s_denom2 = per_layer("s_denom2")
        s_attnT = per_layer("s_attnT")
        s_side = per_layer("s_side")
        s_side_hi = per_layer("s_side_hi")
        s_side_lo = per_layer("s_side_lo")
        s_proj = per_layer("s_proj")
        s_self = per_layer("s_self")
        s_biased = per_layer("s_biased")
        s_self_biased = per_layer("s_self_biased")
        s_proj_hi = per_layer("s_proj_hi")
        s_proj_lo = per_layer("s_proj_lo")
        s_gather = per_layer("s_gather")
        s_whole = per_layer("s_whole")
        s_stats = per_layer("s_stats")
        s_moments = per_layer("s_moments")
        s_veps = per_layer("s_veps")
        s_rstd = per_layer("s_rstd")
        s_nbias = per_layer("s_nbias")
        s_normed = per_layer("s_normed")
        s_normedT = sem("s_normedT")
        s_relu = sem("s_relu")
        s_scaled = sem("s_scaled")
        s_shifted = sem("s_shifted")
        s_y = sem("s_y")
        s_y_stats = sem("s_y_stats")
        s_y_moments = sem("s_y_moments")
        s_y_rstd = sem("s_y_rstd")
        s_y_nbias = sem("s_y_nbias")
        s_y_only = sem("s_y_only")
        s_o = sem("s_o")

        def live(i, b):
            return not isinstance(i, int) or 0 <= b < G

        def done(eng, s, b):
            if not isinstance(b, int) or b >= 0:
                eng.wait_ge(s, b + 1)

        def moved(eng, pair, b, slot):
            if not isinstance(b, int) or b >= 0:
                eng.wait_ge(pair[slot], (b - slot) * 8 + 16)

        def done_apart(eng, s, b):
            count = b + 1 if isinstance(b, int) else eng.snap(b + 1)
            eng.wait_ge(s_setup, 5)
            eng.wait_ge(s, count)

        def low_projections(op, eng, k, b):
            done(eng, s_proj_hi[k], b)
            op.tensor_tensor(proj_split[k][:, LO], proj[k][:, UP:LOW + 1, :],
                             proj_split[k][:, HI].bitcast(F32), ALU.subtract).then_inc(s_proj_lo[k], 1)

        def gain_and_shift(op, eng, b):
            done(eng, s_normed[1], b)
            op.tensor_tensor(scaled[:], normed[1][:], gain2[:], ALU.mult).then_inc(s_scaled, 1)
            done(eng, s_scaled, b)
            done(eng, s_y, b - 1)
            op.tensor_tensor(shifted[:], scaled[:], shift2[:], ALU.add).then_inc(s_shifted, 1)

        def last_graph(i):
            return isinstance(i, int) and i == G + 1

        def after_last_graph(i):
            return isinstance(i, int) and i == G + 2

        def by_vector(i, k, b):
            return isinstance(i, int) and (0 <= b < 2 if k == 0 else G - 2 <= b < G)

        def run(eng, iteration):
            for i in range(FIRST):
                iteration(i, i % 2)
            with eng.Fori(FIRST, LAST - UNROLL + 1, UNROLL) as i:
                for n in range(UNROLL):
                    iteration(i + n, n % 2)
            for i in range(LAST, END):
                iteration(i, i % 2)

        def col(tile, slot, k):
            return tile[:, slot, k:k + 1]

        block = ctx.enter_context(nc.Block())

        @block.sync
        def _(sp):
            for b in (0, 1, 2):
                if b == 2:
                    done(sp, s_lo[0], 0)
                sp.dma_start(xt_raw[:, b % 2], xT[b]).then_inc(s_xt[b % 2], 16)
                if b == 0:
                    for which in range(3):
                        sp.dma_start(w_raw[:, 0, which], WT[0, :, which]).then_inc(s_w[0][which], 16)
                if b < 2:
                    sp.dma_start(adj_tile[0][:, b], adj[b]).then_inc(s_adj[0][b], 16)
                if b == 1:
                    sp.dma_start(bias_all[:, 0], bias[0].partition_broadcast(P)).then_inc(s_bias[0], 16)
                    for which in range(3):
                        sp.dma_start(w_raw[:, 1, which], WT[1, :, which]).then_inc(s_w[1][which], 16)
                    sp.dma_start(bias_all[:, 1], bias[1].partition_broadcast(P)).then_inc(s_bias[1], 16)
                    sp.dma_start(gain1[:], gain_cols).then_inc(s_const, 16)
                    sp.dma_start(shift1[:], shift_cols).then_inc(s_const, 16)
                    sp.dma_start(gain2[:], gain_row.partition_broadcast(P)).then_inc(s_const, 16)
                    sp.dma_start(shift2[:], shift_row.partition_broadcast(P)).then_inc(s_const, 16)
            done(sp, s_diag[0], 0)
            sp.dma_start(adj_tile[0][:, 0], adj[2]).then_inc(s_adj[0][0], 16)

            def iteration(i, p):
                q = 1 - p
                if live(i, i + 3):
                    done(sp, s_lo[0], i + 1)
                    sp.dma_start(xt_raw[:, q], xT[i + 3]).then_inc(s_xt[q], 16)
                if live(i, i):
                    done(sp, s_attn[1], i - 2)
                    sp.dma_start(adj_tile[1][:, p], adj[i]).then_inc(s_adj[1][p], 16)
                if live(i, i - 2):
                    done(sp, s_y, i - 4)
                    sp.dma_start(xn[:, p], x[i - 2]).then_inc(s_xn[p], 16)
                if live(i, i + 3):
                    done(sp, s_attn[0], i + 1)
                    sp.dma_start(adj_tile[0][:, q], adj[i + 3]).then_inc(s_adj[0][q], 16)
                if live(i, i - 4):
                    done(sp, s_o, i - 4)
                    sp.dma_start(out[i - 4], o[:, p]).then_inc(s_out[p], 16)

            run(sp, iteration)
            moved(sp, s_out, G - 2, 0)
            moved(sp, s_out, G - 1, 1)

        @block.tensor
        def _(pe):
            def score_step(k, slot, n):
                return nc.tensor.matmul(p_score[k][:, HI:LO + 1, :], hT[k][:, slot, HI, n, :],
                                        hT[k][:, slot, HI:LO + 1, n, :], start=(n == 0), stop=(n == C - 1))

            def project_step(k, slot, which, n):
                c, (mv, st) = n // 3, TERMS[n % 3]
                return nc.tensor.matmul(p_proj[:, which, 0:D], hT[k][:, slot, st, c, :],
                                        w[:, k, which, mv, c, :], start=(n == 0), stop=(n == 8))

            def project_and_score(i, k, b, slot, other, b_other, slot_other, b_before, b_gather=None):
                project, score = live(i, b), live(i, b_other)
                if project:
                    before, b_last = (1 - k, b_before) if live(i, b_before) else (k, b - 1)
                    done(pe, s_biased[before], b_last)
                if score:
                    done(pe, s_lo[other], b_other)
                for n in range(18):
                    if project:
                        if isinstance(b, int) and b == 0 and n % 3 == 0:
                            pe.wait_ge(s_w_lo[k], n // 3 + 1)
                        last = project_step(k, slot, UP + n // 9, n % 9)
                    if score and n % 2 == 0 and n // 2 < C:
                        step = score_step(other, slot_other, n // 2)
                        if n // 2 == C - 1:
                            step.then_inc(s_parts[other], 1)
                    if b_gather is not None and n == 16:
                        gather(k, b_gather)
                    if score and n == 14:
                        done(pe, s_cross[other], b_other)
                        nc.tensor.matmul(p_score[other][:, HI, :], cross[other][:], ident_r[:], start=False,
                                         stop=True, skip_group_check=True).then_inc(s_score[other], 1)
                if project:
                    last.then_inc(s_proj[k], 1)
                    done(pe, s_attn[k], b)
                    nc.tensor.transpose(p_attnT, A[k][:], ident[:]).then_inc(s_attnT[k], 1)
                    if isinstance(b, int) and b == 0:
                        pe.wait_ge(s_w_lo[k], 3 * C)
                    for n in range(9):
                        last = project_step(k, slot, SELF, n)
                    last.then_inc(s_self[k], 1)

            def gather(k, b):
                done(pe, s_side_lo[k], b)
                done(pe, s_proj_lo[k], b)
                for side in (UP, LOW):
                    for n, (mv, st) in enumerate(TERMS):
                        last = nc.tensor.matmul(p_gather[k][:, 0:D], AT_split[k][:, st, side, :],
                                                proj_split[k][:, mv, side, :],
                                                start=(side == UP and n == 0), stop=(side == LOW and n == 2))
                last.then_inc(s_gather[k], 1)

            pe.wait_ge(s_setup, 5)
            pe.wait_ge(s_ident_r, 1)
            project_and_score(-1, 1, -3, 1, 0, 0, 0, -1)

            def iteration(i, p):
                q = 1 - p
                if last_graph(i):
                    project_and_score(i, 1, i - 2, p, 1, i - 2, p, i, i - 3)
                    return
                project_and_score(i, 0, i, p, 1, i - 2, p, i - 3)
                if live(i, i - 3):
                    gather(1, i - 3)
                if live(i, i - 1):
                    done(pe, s_normed[0], i - 1)
                    for c in range(C):
                        last = nc.tensor.transpose(p_gather[0][:, c * P:(c + 1) * P],
                                                   normed[0][:, c * P:(c + 1) * P], ident[:])
                    last.then_inc(s_normedT, 1)
                project_and_score(i, 1, i - 2, p, 0, i + 1, q, i)
                if live(i, i):
                    done(pe, s_lo[1], i - 1)
                    gather(0, i)

            run(pe, iteration)

        @block.vector
        def _(dve):
            def normalise_rows(k, b, slot, b_y, slot_y):
                layer, final = b is not None, b_y is not None
                if layer:
                    done(dve, s_gather[k], b)
                    done(dve, s_diag[k], b)
                    if k == 1:
                        done(dve, s_normed[k], b - 1)
                    nc.vector.scalar_tensor_tensor(
                        out=gathered[k][:], in0=proj[k][:, SELF, :], scalar=col(rows[k], slot, DIAG),
                        in1=p_gather[k][:, 0:D], op0=ALU.mult, op1=ALU.add).then_inc(s_whole[k], 1)
                if final:
                    done(dve, s_shifted, b_y)
                    moved(dve, s_xn, b_y, slot_y)
                    done(dve, s_o, b_y - 1)
                    nc.vector.scalar_tensor_tensor(out=y[:], in0=shifted[:], scalar=0.0,
                                                   in1=xn[:, slot_y, :], op0=ALU.max,
                                                   op1=ALU.add).then_inc(s_y, 1)
                if layer:
                    done(dve, s_whole[k], b)
                    nc.vector.bn_stats(stats6[k][:, LAYER], gathered[k][:]).then_inc(s_stats[k], 1)
                if final:
                    done(dve, s_y, b_y)
                    nc.vector.bn_stats(stats6[k][:, FINAL], y[:]).then_inc(s_y_stats, 1)
                if layer:
                    done_apart(dve, s_stats[k], b)
                    nc.vector.bn_aggr(moments[k][:, LAYER], stats6[k][:, LAYER]).then_inc(s_moments[k], 1)
                if final:
                    done_apart(dve, s_y_stats, b_y)
                    nc.vector.bn_aggr(moments[k][:, FINAL], stats6[k][:, FINAL]).then_inc(s_y_moments, 1)
                which = slice(FINAL if not layer else LAYER, FINAL + 1 if final else LAYER + 1)
                last = s_y_only if not layer else s_veps[k]
                if layer:
                    done(dve, s_moments[k], b)
                    done(dve, s_denom2[k], b)
                if final:
                    done(dve, s_y_moments, b_y)
                nc.vector.scalar_tensor_tensor(
                    out=veps[k][:, which], in0=eps_units[k][:, slot, which], scalar=GNN_EPS,
                    in1=moments[k][:, which, 1], op0=ALU.mult, op1=ALU.add)
                nc.vector.tensor_scalar(neg_mean[k][:, which], moments[k][:, which, 0], -1.0, None,
                                        ALU.mult).then_inc(last, 1)

            def add_bias(k, b, sides_too):
                if isinstance(b, int) and b == 0:
                    dve.wait_ge(s_bias[k], 16)
                if sides_too:
                    done(dve, s_proj[k], b)
                    nc.vector.tensor_tensor(proj[k][:, UP:LOW + 1, :], p_proj[:, UP:LOW + 1, 0:D],
                                            bias_all[:, k, UP:LOW + 1, :], ALU.add).then_inc(s_biased[k], 1)
                else:
                    done(dve, s_self[k], b)
                    nc.vector.tensor_tensor(proj[k][:, SELF, :], p_proj[:, SELF, 0:D],
                                            bias_all[:, k, SELF, :], ALU.add).then_inc(s_self_biased[k], 1)

            def scaled_scores(k, b, slot):
                nc.vector.tensor_tensor_reduce(U[k][:], p_score[k][:, HI, :], cross[k][:].bitcast(F32), -SCALE,
                                               MOST, ALU.add, ALU.min,
                                               col(rows[k], slot, NEGMAX)).then_inc(s_negmax[k], 1)

            def mask(k, b, slot):
                done(dve, s_exp[k], b)
                moved(dve, s_adj[k], b, slot)
                nc.vector.tensor_tensor_reduce(A[k][:], E[k], adj_tile[k][:, slot, :], 1.0, 0.0, ALU.mult,
                                               ALU.add, col(rows[k], slot, ADJSUM)).then_inc(s_attn[k], 1)

            def cut_sides(k, b, slot):
                done(dve, s_attnT[k], b)
                nc.vector.tensor_tensor(AT[k][:], p_attnT.unsqueeze(1).broadcast_to([P, 2, N]), sides[:],
                                        ALU.mult).then_inc(s_side[k], 1)
                nc.vector.tensor_tensor_reduce(diag_scratch[k][:], p_attnT, ident[:], 1.0, 0.0, ALU.mult,
                                               ALU.add, col(rows[k], slot, DIAG)).then_inc(s_diag[k], 1)

            def low_weights(k, which):
                dve.wait_ge(s_w_hi[k][which], 1)
                nc.vector.tensor_tensor(w[:, k, which, LO], w_raw[:, k, which],
                                        w[:, k, which, HI].bitcast(F32), ALU.subtract).then_inc(s_w_lo[k], C)

            dve.wait_ge(s_setup, 5)
            nc.vector.tensor_copy(ident_r[:], ident[:]).then_inc(s_ident_r, 1)
            for k in (0, 1):
                nc.vector.memset(eps_units[k][:], OUT_EPS / GNN_EPS).then_inc(s_eps, 1)
            dve.wait_ge(s_w[0][UP], 16)
            for c in range(C):
                nc.vector.tensor_copy(w[:, 0, UP, HI, c], w_raw[:, 0, UP, c]).then_inc(s_w_hi[0][UP], 1)
                dve.wait_ge(s_w_hi[0][UP], c + 1)
                nc.vector.tensor_tensor(w[:, 0, UP, LO, c], w_raw[:, 0, UP, c],
                                        w[:, 0, UP, HI, c].bitcast(F32), ALU.subtract).then_inc(s_w_lo[0], 1)
            low_weights(0, LOW)
            done(dve, s_score[0], 0)
            scaled_scores(0, 0, 0)
            low_weights(0, SELF)
            mask(0, 0, 0)

            def iteration(i, p):
                q = 1 - p
                if after_last_graph(i):
                    normalise_rows(1, i - 3, q, None, 0)
                if live(i, i - 1) or live(i, i - 4):
                    normalise_rows(0, i - 1 if live(i, i - 1) else None, q,
                                   i - 4 if live(i, i - 4) else None, p)
                if live(i, i):
                    add_bias(0, i, True)
                if live(i, i - 2):
                    done(dve, s_score[1], i - 2)
                if live(i, i):
                    cut_sides(0, i, p)
                if live(i, i - 2):
                    scaled_scores(1, i - 2, p)
                if live(i, i):
                    add_bias(0, i, False)
                if by_vector(i, 0, i):
                    low_projections(nc.vector, dve, 0, i)
                if live(i, i - 2):
                    mask(1, i - 2, p)
                if isinstance(i, int) and i == 1:
                    low_weights(1, LOW)
                if live(i, i - 3) and not last_graph(i) and not after_last_graph(i):
                    normalise_rows(1, i - 3, q, None, 0)
                if after_last_graph(i):
                    gain_and_shift(nc.vector, dve, i - 3)
                if live(i, i - 1):
                    done(dve, s_hi[1], i - 1)
                    nc.vector.tensor_tensor(hT[1][:, q, LO], relu_T, hT[1][:, q, HI].bitcast(F32),
                                            ALU.subtract).then_inc(s_lo[1], 1)
                if live(i, i - 2):
                    add_bias(1, i - 2, True)
                if live(i, i + 1):
                    done(dve, s_score[0], i + 1)
                if live(i, i - 2):
                    cut_sides(1, i - 2, p)
                if last_graph(i):
                    normalise_rows(1, i - 3, q, None, 0)
                if live(i, i + 1):
                    scaled_scores(0, i + 1, q)
                if live(i, i - 2):
                    add_bias(1, i - 2, False)
                if by_vector(i, 1, i - 2):
                    low_projections(nc.vector, dve, 1, i - 2)
                if live(i, i + 1):
                    mask(0, i + 1, q)
                if isinstance(i, int) and i < 2:
                    low_weights(1, UP if i == 0 else SELF)

            run(dve, iteration)

        @block.scalar
        def _(act):
            def cross_scores(k, b):
                done(act, s_parts[k], b)
                nc.scalar.activation(cross[k][:], p_score[k][:, LO, :], ACT.Copy).then_inc(s_cross[k], 1)

            def exponentials(k, b, slot):
                done(act, s_negmax[k], b)
                nc.scalar.activation(E[k], U[k][:], ACT.Exp, bias=col(rows[k], slot, NEGMAX),
                                     scale=-1.0, accum_out=col(rows[k], slot, EXPSUM)).then_inc(s_exp[k], 1)

            def high_sides(k, b):
                done(act, s_side[k], b)
                nc.scalar.activation(AT_split[k][:, HI], AT[k][:], ACT.Copy).then_inc(s_side_hi[k], 1)

            def high_projections(k, b):
                done(act, s_biased[k], b)
                nc.scalar.activation(proj_split[k][:, HI], proj[k][:, UP:LOW + 1, :],
                                     ACT.Copy).then_inc(s_proj_hi[k], 1)

            def normalise(k, b, count, which, rows_in, rows_out, s_rows):
                done(act, count, b)
                nc.scalar.activation(rows_out, rows_in, ACT.Identity, bias=nbias[k][:, which:which + 1],
                                     scale=rstd[k][:, which:which + 1]).then_inc(s_rows, 1)

            def high_input(b, slot):
                moved(act, s_xt, b, slot)
                done(act, s_self[0], b - 2)
                nc.scalar.activation(hT[0][:, slot, HI], xt_raw[:, slot], ACT.Copy).then_inc(s_hi[0], 1)

            def high_weights(k, which):
                act.wait_ge(s_w[k][which], 16)
                nc.scalar.activation(w[:, k, which, HI], w_raw[:, k, which],
                                     ACT.Copy).then_inc(s_w_hi[k][which], 1)

            high_input(0, 0)
            cross_scores(0, 0)
            high_weights(0, LOW)
            high_weights(0, SELF)
            exponentials(0, 0, 0)

            def iteration(i, p):
                q = 1 - p
                if live(i, i + 1):
                    high_input(i + 1, q)
                if live(i, i - 2):
                    cross_scores(1, i - 2)
                if live(i, i - 1):
                    normalise(0, i - 1, s_nbias[0], LAYER, gathered[0][:], normed[0][:], s_normed[0])
                if live(i, i):
                    high_sides(0, i)
                if live(i, i - 2):
                    exponentials(1, i - 2, p)
                if live(i, i):
                    high_projections(0, i)
                if after_last_graph(i):
                    normalise(1, i - 3, s_nbias[1], LAYER, gathered[1][:], normed[1][:], s_normed[1])
                if live(i, i - 4):
                    moved(act, s_out, i - 6, p)
                    beside = live(i, i - 1)
                    normalise(0, i - 1 if beside else i - G - 1, s_nbias[0] if beside else s_y_nbias, FINAL,
                              y[:], o[:, p, :], s_o)
                if live(i, i + 1):
                    cross_scores(0, i + 1)
                if live(i, i - 1):
                    if isinstance(i, int) and i == 1:
                        act.wait_ge(s_const, 64)
                    done(act, s_normedT, i - 1)
                    for c in range(C):
                        last = nc.scalar.activation(relu_T[:, c, :], relu_T[:, c, :], ACT.Relu,
                                                    bias=shift1[:, c:c + 1], scale=gain1[:, c:c + 1])
                    last.then_inc(s_relu, 1)
                    done(act, s_relu, i - 1)
                    done(act, s_self[1], i - 3)
                    nc.scalar.activation(hT[1][:, q, HI], relu_T, ACT.Copy).then_inc(s_hi[1], 1)
                if live(i, i - 3) and not last_graph(i) and not after_last_graph(i):
                    normalise(1, i - 3, s_nbias[1], LAYER, gathered[1][:], normed[1][:], s_normed[1])
                if live(i, i - 2):
                    high_sides(1, i - 2)
                if live(i, i + 1):
                    exponentials(0, i + 1, q)
                if live(i, i - 2):
                    high_projections(1, i - 2)
                if last_graph(i):
                    normalise(1, i - 3, s_nbias[1], LAYER, gathered[1][:], normed[1][:], s_normed[1])
                if isinstance(i, int) and i == 0:
                    high_weights(1, UP)
                    high_weights(1, LOW)
                if isinstance(i, int) and i == 1:
                    high_weights(1, SELF)

            run(act, iteration)

        @block.gpsimd
        def _(pool):
            def low_sides(k, b):
                done(pool, s_side_hi[k], b)
                nc.gpsimd.tensor_tensor(AT_split[k][:, LO], AT[k][:], AT_split[k][:, HI].bitcast(F32),
                                        ALU.subtract).then_inc(s_side_lo[k], 1)

            def deviation(k, b, which, s_v, s_r, s_n):
                done(pool, s_v, b)
                nc.gpsimd.tensor_tensor(rstd[k][:, which], veps[k][:, which], neg_half[:, which],
                                        ALU.pow).then_inc(s_r, 1)
                done(pool, s_r, b)
                nc.gpsimd.tensor_tensor(nbias[k][:, which], neg_mean[k][:, which], rstd[k][:, which],
                                        ALU.mult).then_inc(s_n, 1)

            def denominator(k, b, slot):
                r = rows[k]
                nc.gpsimd.tensor_scalar(col(r, slot, DENOM), col(r, slot, EXPSUM), ATTN_EPS,
                                        col(r, slot, ADJSUM), ALU.mult, ALU.add).then_inc(s_denom[k], 1)
                done(pool, s_denom[k], b)
                nc.gpsimd.tensor_tensor(eps_units[k][:, slot, LAYER:LAYER + 1], col(r, slot, DENOM),
                                        col(r, slot, DENOM), ALU.mult).then_inc(s_denom2[k], 1)

            def low_input(b, slot):
                done(pool, s_hi[0], b)
                nc.gpsimd.tensor_tensor(hT[0][:, slot, LO], xt_raw[:, slot], hT[0][:, slot, HI].bitcast(F32),
                                        ALU.subtract).then_inc(s_lo[0], 1)

            nc.gpsimd.memset(ident[:], 0.0).then_inc(s_setup, 1)
            nc.gpsimd.memset(sides[:], 1.0).then_inc(s_setup, 1)
            nc.gpsimd.memset(neg_half[:], -0.5)
            pool.wait_ge(s_setup, 2)
            nc.gpsimd.affine_select(out=ident[:], in_=ident[:], compare_op=ALU.not_equal, fill=1.0, base=0,
                                    pattern=[[-1, P]], channel_multiplier=1).then_inc(s_setup, 1)
            nc.gpsimd.affine_select(out=sides[:, UP, :], in_=sides[:, UP, :], compare_op=ALU.is_gt, fill=0.0,
                                    base=0, pattern=[[-1, P]], channel_multiplier=1).then_inc(s_setup, 1)
            nc.gpsimd.affine_select(out=sides[:, LOW, :], in_=sides[:, LOW, :], compare_op=ALU.is_gt,
                                    fill=0.0, base=0, pattern=[[1, P]],
                                    channel_multiplier=-1).then_inc(s_setup, 1)
            pool.wait_ge(s_setup, 5)
            low_input(0, 0)
            pool.wait_ge(s_eps, 2)
            done(pool, s_attn[0], 0)
            denominator(0, 0, 0)

            def iteration(i, p):
                q = 1 - p
                if live(i, i - 3) and not by_vector(i, 1, i - 3):
                    low_projections(nc.gpsimd, pool, 1, i - 3)
                if after_last_graph(i):
                    deviation(1, i - 3, slice(LAYER, LAYER + 1), s_veps[1], s_rstd[1], s_nbias[1])
                if live(i, i - 1):
                    deviation(0, i - 1, slice(LAYER, FINAL + 1 if live(i, i - 4) else LAYER + 1), s_veps[0],
                              s_rstd[0], s_nbias[0])
                elif live(i, i - 4):
                    deviation(0, i - G - 1, slice(FINAL, FINAL + 1), s_y_only, s_y_rstd, s_y_nbias)
                if live(i, i + 1):
                    low_input(i + 1, q)
                if live(i, i - 2):
                    done(pool, s_attn[1], i - 2)
                if live(i, i):
                    low_sides(0, i)
                if live(i, i - 2):
                    denominator(1, i - 2, p)
                if live(i, i) and not by_vector(i, 0, i):
                    low_projections(nc.gpsimd, pool, 0, i)
                if last_graph(i):
                    low_sides(1, i - 2)
                if live(i, i - 3) and not after_last_graph(i):
                    deviation(1, i - 3, slice(LAYER, LAYER + 1), s_veps[1], s_rstd[1], s_nbias[1])
                    if isinstance(i, int) and i == 3:
                        pool.wait_ge(s_const, 64)
                    gain_and_shift(nc.gpsimd, pool, i - 3)
                if live(i, i + 1):
                    done(pool, s_attn[0], i + 1)
                if live(i, i - 2) and not last_graph(i):
                    low_sides(1, i - 2)
                if live(i, i + 1):
                    denominator(0, i + 1, q)

            run(pool, iteration)


def kernel(x, adj, L0_gnn_Wl, L0_gnn_bl, L0_gnn_Ws, L0_gnn_bs, L0_gnn_Wr, L0_gnn_br, L0_gnn_ln_w, L0_gnn_ln_b):
    import numpy as np
    import concourse.bacc as bacc
    from concourse.bass_utils import run_bass_kernel_spmd

    G, N, D = x.shape
    C = D // P
    W = np.stack([L0_gnn_Wl, L0_gnn_Wr, L0_gnn_Ws], axis=1)
    W = W.reshape(2, 3, D, C, P).transpose(0, 4, 1, 3, 2)
    arrays = {
        "xT": np.asarray(x).reshape(G, N, C, P).transpose(0, 3, 2, 1),
        "x": x,
        "adj": adj,
        "WT": W,
        "bias": np.stack([L0_gnn_bl, L0_gnn_br, L0_gnn_bs], axis=1),
        "gain_cols": np.asarray(L0_gnn_ln_w)[0].reshape(C, P).T,
        "shift_cols": np.asarray(L0_gnn_ln_b)[0].reshape(C, P).T,
        "gain_row": np.asarray(L0_gnn_ln_w)[1],
        "shift_row": np.asarray(L0_gnn_ln_b)[1],
    }
    arrays = {name: np.ascontiguousarray(a) for name, a in arrays.items()}
    nc = bacc.Bacc("TRN2", target_bir_lowering=False, num_devices=1)
    args = [nc.dram_tensor(name, a.shape, mybir.dt.from_np(a.dtype), kind="ExternalInput").ap()
            for name, a in arrays.items()]
    args.append(nc.dram_tensor("out", (G, N, D), F32, kind="ExternalOutput").ap())
    graph_block(nc, *args)
    r = run_bass_kernel_spmd(nc, [arrays], core_ids=[0])
    return r.results[0]["out"]
```
